# Optimizing a Trainium2 kernel written in Bass

```python
import numpy as np
import jax
import jax.numpy as jnp

def _softmax(x, axis=-1):
    return jax.nn.softmax(x, axis=axis)

def _gelu(x):
    return jax.nn.gelu(x, approximate=True)

def _silu(x):
    return jax.nn.silu(x)

def _sigmoid(x):
    return jax.nn.sigmoid(x)

def _layernorm(x, axis=-1, eps=1e-05):
    m = jnp.mean(x, axis=axis, keepdims=True)
    v = jnp.var(x, axis=axis, keepdims=True)
    return (x - m) / jnp.sqrt(v + eps)

def _scatter_add(tgt, idx, src, axis=0):
    return tgt.at[idx].add(src)

def _segment_sum(src, seg, n):
    return jax.ops.segment_sum(src, seg, n)
kernel_name = 'mk_seq_postln_d1_jaxref_r8_a3535d'

def setup_inputs(seed: int=0):
    np.random.seed(seed)
    _w = jnp.asarray

    def _L0_attn_setup():
        import jax, jax.numpy as jnp
        import numpy as np
        H = 16
        D = 128
        M = 16
        ROPE = 64
        THETA = 10000.0
        WIN = 64
        CAP = 50.0
        G = 4
        HID = 256
        QC = 64
        INTER = 256

        def rope_cache(t):
            inv = 1.0 / THETA ** (jnp.arange(0, ROPE, 2, dtype=jnp.float32) / ROPE)
            ang = jnp.arange(t, dtype=jnp.float32)[:, None] * inv[None, :]
            return (jnp.cos(ang), jnp.sin(ang))

        def apply_partial_rope(x, cos, sin):
            x1 = x[..., :ROPE // 2]
            x2 = x[..., ROPE // 2:ROPE]
            rest = x[..., ROPE:]
            return jnp.concatenate([x1 * cos - x2 * sin, x1 * sin + x2 * cos, rest], axis=-1)

        def rmsnorm(x, w, eps=1e-06):
            return x * jax.lax.rsqrt(jnp.mean(x * x, axis=-1, keepdims=True) + eps) * w

        def attend(scores, mask, sink, v, sub):
            b, h, t, _ = scores.shape
            logits = jnp.where(mask, scores, jnp.float32(-1e+30))
            sink_col = jnp.broadcast_to(sink[None, :, None, None], (b, h, t, 1))
            probs = jax.nn.softmax(jnp.concatenate([logits, sink_col], axis=-1), axis=-1)[..., :-1]
            return jnp.einsum(sub, probs, v)
        key = jax.random.key(seed)
        ks = jax.random.split(key, 12)
        s = 0.02
        return {'h': jax.random.normal(ks[0], (2, 256, HID), dtype=jnp.float32), 'Wq_c': jax.random.normal(ks[1], (HID, QC), dtype=jnp.float32) * s, 'Wq_up': jax.random.normal(ks[2], (QC, H * D), dtype=jnp.float32) * s, 'Wk': jax.random.normal(ks[3], (HID, D), dtype=jnp.float32) * s, 'Wv': jax.random.normal(ks[4], (HID, D), dtype=jnp.float32) * s, 'W_comp': jax.random.normal(ks[5], (M * HID, D), dtype=jnp.float32) * s, 'q_norm_w': jnp.ones((D,), dtype=jnp.float32), 'k_norm_w': jnp.ones((D,), dtype=jnp.float32), 'sink': jnp.zeros((H,), dtype=jnp.float32), 'Wg': jax.random.normal(ks[6], (G, H // G * D, INTER), dtype=jnp.float32) * s, 'Wo': jax.random.normal(ks[7], (G * INTER, HID), dtype=jnp.float32) * s}
    _L0_attn_in = _L0_attn_setup()

    def _L0_ffn_setup():
        import jax, jax.numpy as jnp
        import numpy as np
        B, S, D_IN, D_OUT = (4, 256, 256, 256)
        EPS = 1e-10
        key = jax.random.key(seed)
        kx, kw, kb = jax.random.split(key, 3)
        x = jax.random.normal(kx, (B, S, D_IN), dtype=jnp.float32)
        weight = jax.random.normal(kw, (D_OUT, D_IN), dtype=jnp.float32) * 0.02
        bias = jax.random.normal(kb, (D_OUT,), dtype=jnp.float32) * 0.02
        return {'x': x, 'weight': weight, 'bias': bias}
    _L0_ffn_in = _L0_ffn_setup()
    _d = {'L0_attn_h': _L0_attn_in['h'], 'L0_attn_Wq_c': _L0_attn_in['Wq_c'], 'L0_attn_Wq_up': _L0_attn_in['Wq_up'], 'L0_attn_Wk': _L0_attn_in['Wk'], 'L0_attn_Wv': _L0_attn_in['Wv'], 'L0_attn_W_comp': _L0_attn_in['W_comp'], 'L0_attn_q_norm_w': _L0_attn_in['q_norm_w'], 'L0_attn_k_norm_w': _L0_attn_in['k_norm_w'], 'L0_attn_sink': _L0_attn_in['sink'], 'L0_attn_Wg': _L0_attn_in['Wg'], 'L0_attn_Wo': _L0_attn_in['Wo'], 'L0_ffn_weight': _L0_ffn_in['weight'], 'L0_ffn_bias': _L0_ffn_in['bias']}
    _x0 = _d['L0_attn_h']
    _d['L0_attn_h'] = jax.random.normal(jax.random.fold_in(jax.random.key(seed), 1), (2, 1024, 256), dtype=_x0.dtype)
    del _x0
    return _d

def reference(L0_attn_h, L0_attn_Wq_c, L0_attn_Wq_up, L0_attn_Wk, L0_attn_Wv, L0_attn_W_comp, L0_attn_q_norm_w, L0_attn_k_norm_w, L0_attn_sink, L0_attn_Wg, L0_attn_Wo, L0_ffn_weight, L0_ffn_bias):

    def _L0_attn_ref(h, Wq_c, Wq_up, Wk, Wv, W_comp, q_norm_w, k_norm_w, sink, Wg, Wo):
        import jax, jax.numpy as jnp
        import numpy as np
        H = 16
        D = 128
        M = 16
        ROPE = 64
        THETA = 10000.0
        WIN = 64
        CAP = 50.0
        G = 4
        HID = 256
        QC = 64
        INTER = 256

        def rope_cache(t):
            inv = 1.0 / THETA ** (jnp.arange(0, ROPE, 2, dtype=jnp.float32) / ROPE)
            ang = jnp.arange(t, dtype=jnp.float32)[:, None] * inv[None, :]
            return (jnp.cos(ang), jnp.sin(ang))

        def apply_partial_rope(x, cos, sin):
            x1 = x[..., :ROPE // 2]
            x2 = x[..., ROPE // 2:ROPE]
            rest = x[..., ROPE:]
            return jnp.concatenate([x1 * cos - x2 * sin, x1 * sin + x2 * cos, rest], axis=-1)

        def rmsnorm(x, w, eps=1e-06):
            return x * jax.lax.rsqrt(jnp.mean(x * x, axis=-1, keepdims=True) + eps) * w

        def attend(scores, mask, sink, v, sub):
            b, h, t, _ = scores.shape
            logits = jnp.where(mask, scores, jnp.float32(-1e+30))
            sink_col = jnp.broadcast_to(sink[None, :, None, None], (b, h, t, 1))
            probs = jax.nn.softmax(jnp.concatenate([logits, sink_col], axis=-1), axis=-1)[..., :-1]
            return jnp.einsum(sub, probs, v)
        b, t, _ = h.shape
        cos, sin = rope_cache(t)
        q = (h @ Wq_c @ Wq_up).reshape(b, t, H, D).transpose(0, 2, 1, 3)
        q = rmsnorm(apply_partial_rope(q, cos, sin), q_norm_w)
        k_sw = rmsnorm(apply_partial_rope(h @ Wk, cos, sin), k_norm_w)
        v_sw = h @ Wv
        nb = t // M
        ck = rmsnorm(h.reshape(b, nb, M * HID) @ W_comp, k_norm_w)
        scale = 1.0 / jnp.sqrt(jnp.float32(D))
        pos = jnp.arange(t)
        blk_end = jnp.arange(nb) * M + (M - 1)
        valid = blk_end[None, :] < pos[:, None]
        c_scores = jnp.einsum('bhtd,bnd->bhtn', q, ck) * scale
        c_out = attend(c_scores, valid[None, None], sink, ck, 'bhtn,bnd->bhtd')
        sw_scores = jnp.einsum('bhtd,bsd->bhts', q, k_sw) * scale
        sw_scores = CAP * jnp.tanh(sw_scores / CAP)
        sw_mask = (pos[None, :] <= pos[:, None]) & (pos[:, None] - pos[None, :] < WIN)
        sw_out = attend(sw_scores, sw_mask[None, None], sink, v_sw, 'bhts,bsd->bhtd')
        ao = (c_out + sw_out).transpose(0, 2, 1, 3).reshape(b, t, G, H // G * D)
        inter = jnp.einsum('btgf,gfi->btgi', ao, Wg)
        return inter.reshape(b, t, G * INTER) @ Wo

    def _L0_ffn_ref(x, weight, bias):
        import jax, jax.numpy as jnp
        import numpy as np
        B, S, D_IN, D_OUT = (4, 256, 256, 256)
        EPS = 1e-10
        scale = jnp.mean(jnp.abs(weight))
        w_t = jnp.clip(jnp.round(weight / (scale + EPS)), -1.0, 1.0)
        w_ste = weight + jax.lax.stop_gradient(w_t * scale - weight)
        return jnp.einsum('bsi,oi->bso', x, w_ste) + bias
    x = L0_attn_h
    x = _layernorm(x + _L0_attn_ref(x, L0_attn_Wq_c, L0_attn_Wq_up, L0_attn_Wk, L0_attn_Wv, L0_attn_W_comp, L0_attn_q_norm_w, L0_attn_k_norm_w, L0_attn_sink, L0_attn_Wg, L0_attn_Wo), axis=-1)
    x = _layernorm(x + _L0_ffn_ref(x, L0_ffn_weight, L0_ffn_bias), axis=-1)
    return x

_drawn_inputs = setup_inputs


def setup_inputs(seed=0):
    import zlib

    import numpy as np

    out = dict(_drawn_inputs(seed))
    spreads = {'L0_attn_q_norm_w': (1.0, 0.6), 'L0_attn_k_norm_w': (1.0, 0.6), 'L0_attn_sink': (0.0, 2.0)}
    factors = {'L0_attn_Wk': 3.495, 'L0_attn_Wv': 2.779, 'L0_ffn_bias': 2.848}
    for name, (base, spread) in spreads.items():
        noise = np.random.default_rng([zlib.crc32(name.encode()), seed]).standard_normal(out[name].shape)
        drawn = base * np.exp(spread * noise) if base else spread * noise
        out[name] = jnp.asarray(drawn.astype(out[name].dtype))
    for name, factor in factors.items():
        out[name] = (out[name] * factor).astype(out[name].dtype)
    return out
```

```python
from contextlib import ExitStack

import concourse.bass as bass
import numpy as np
from concourse import mybir

BATCH, SEQ, HID = 2, 1024, 256
HEADS, D, QC = 16, 128, 64
BLK, WIN = 16, 64
ROPE = 64
GROUPS, INTER = 4, 256
CAP = 50.0
P = 128
NT = BATCH * SEQ // P
TPB = SEQ // P
NBLK = SEQ // BLK
PAIRS = HEADS // 2
KC = HID // P
VW = D + 1
VS = D + 2
SPAN = WIN + SEQ
SCALE = float(D) ** -0.5
TAB = 2 * ROPE
MASKED = -1e30


def shape_tables():
    inv = np.float32(1.0) / np.float32(10000.0) ** (np.arange(0, ROPE, 2, dtype=np.float32) / np.float32(ROPE))
    ang = np.arange(SEQ, dtype=np.float32)[:, None] * inv[None, :].astype(np.float32)
    cos, sin = np.cos(ang), np.sin(ang)
    rope = np.concatenate([cos, cos, -sin, sin], 1).astype(np.float32)
    rope = rope.reshape(TPB, P, TAB).transpose(1, 0, 2).copy()
    t = np.arange(SEQ)
    end = np.arange(NBLK) * BLK + BLK - 1
    block = np.where(end[None] < t[:, None], 0.0, MASKED).astype(np.float32)
    block = block.reshape(TPB, P, NBLK).transpose(1, 0, 2).copy()
    p, q = np.arange(P)[:, None], np.arange(WIN)[None]
    usual = ((p > q) & (p <= q + WIN)).astype(np.float32)
    first = usual * (p >= WIN)
    window = np.stack([first] + [usual] * (TPB - 1), 1).astype(np.float32)
    return rope, block, np.ascontiguousarray(window)


def build(nc, h, wqc, wqup, wk, wv, wcomp, qnw, knw, sink, wg, wo, fw, fb, rope_t, block_t, window_t, out):
    f32, bf16, i32 = mybir.dt.float32, mybir.dt.bfloat16, mybir.dt.int32
    ALU, ACT, AX = mybir.AluOpType, mybir.ActivationFunctionType, mybir.AxisListType
    ds = bass.ds

    h_v = h.rearrange("b (j p) c -> p (b j) c", p=P)
    out_v = out.rearrange("b s c -> (b s) c")

    ctx = ExitStack()
    with ctx:
        def sb(name, shape, dt=f32):
            return ctx.enter_context(nc.sbuf_tensor(name, shape, dt))

        def sem(name):
            return ctx.enter_context(nc.semaphore(name))

        H = sb("H", [P, NT, HID])
        ident, identb = sb("ident", [P, P]), sb("identb", [P, P], bf16)
        ones = sb("ones", [P, P])
        rope_s = sb("rope_s", [P, TPB, TAB])
        block_f, block_b = sb("block_f", [P, TPB, NBLK]), sb("block_b", [P, TPB, NBLK], bf16)
        window_s = sb("window_s", [P, TPB, WIN])
        wqup_s = sb("wqup_s", [QC, HEADS * D])
        xcT = sb("xcT", [QC, (NT + 1) * P])
        kT = sb("kT", [P, BATCH, SPAN])
        V = sb("V", [P, 2 * NT, VS])
        ckTs = sb("ckTs", [P, BATCH, NBLK])
        ckTv = sb("ckTv", [P, BATCH, NBLK])
        Weff = sb("Weff", [P, HEADS, HID])
        CW = sb("CW", [P, BATCH, PAIRS, HID])
        wfT = sb("wfT", [P, KC, HID])
        fb_s = sb("fb_s", [P, HID])
        sinkb = sb("sinkb", [P, HEADS])
        e0, e1, skp, skm = (sb(n, [P, PAIRS]) for n in ("e0", "e1", "skp", "skm"))
        qw, kw, wqk = (sb(n, [P, 1]) for n in ("qw", "kw", "wqk"))

        room_h, room_comp, room_wg, room_wgT = (sb(n, [P, w]) for n, w in (
            ("room_h", KC * BATCH * SPAN), ("room_comp", BLK * KC * D),
            ("room_wg", HEADS * INTER), ("room_wgT", KC * HEADS * P)))
        hT = room_h[:, :].rearrange("p (k b s) -> p k b s", k=KC, b=BATCH)
        wcomp_s = room_comp[:, :].rearrange("p (m d) -> p m d", d=D)
        wg_s = room_wg[:, :].rearrange("p (f i) -> p f i", i=INTER)
        wgT = room_wgT[:, :].rearrange("p (k f) -> p k f", k=KC)
        wqc_s, wk_s, wv_s = sb("wqc_s", [P, KC, QC]), sb("wk_s", [P, KC, D]), sb("wv_s", [P, KC, D])
        room_wo, room_K = sb("room_wo", [P, GROUPS * KC * HID]), sb("room_K", [P, (NT + 1) * D])
        wo_s = room_wo[:, :].rearrange("p (k n) -> p k n", n=HID)
        K = room_K[:, :].rearrange("p (t d) -> p t d", d=D)
        fw_s, fw_a, fw_b = (sb(n, [P, KC, HID]) for n in ("fw_s", "fw_a", "fw_b"))
        ckr = sb("ckr", [P, P])
        fsum, fscale, fthr, fthn = (sb(n, [P, 1]) for n in ("fsum", "fscale", "fthr", "fthn"))

        def part(room, start, pattern, size=HEADS * D, **axes):
            return room[:, start:start + size].rearrange(pattern, **axes)

        sq = part(room_K, 0, "p (a d) -> p a d", d=D)
        sqk = part(room_comp, 0, "p (a d) -> p a d", d=D)
        rt1, rt2 = sb("rt1", [P, HEADS, ROPE]), sb("rt2", [P, HEADS, ROPE])
        xcF = sb("xcF", [QC, P])
        kTw = sb("kTw", [P, P + WIN])
        th = part(room_comp, 0, "p (c a q) -> p c a q", c=2, q=WIN)
        E = part(room_comp, 2048, "p (c a q) -> p c a q", c=2, q=WIN)
        Pm = part(room_wg, 0, "p (c a q) -> p c a q", c=2, q=WIN)
        ao = part(room_wg, 2048, "p (c a d) -> p c a d", c=2, d=D)
        aoT = part(room_wgT, 0, "p (a r c q) -> p a r c q", c=2, r=2, q=WIN)
        qs = part(room_wgT, 2048, "p (a d) -> p a d", d=D)
        qT = part(room_h, 0, "p (a q) -> p a q", q=P)
        Cs = part(room_h, 2048, "p (a n) -> p a n", HEADS * NBLK, n=NBLK)
        Ec = part(room_h, 3072, "p (a n) -> p a n", HEADS * NBLK, n=NBLK)
        Pn = part(room_wo, 0, "p (a n) -> p a n", HEADS * NBLK, n=NBLK)
        PcT = part(room_wo, 1024, "p (a q) -> p a q", PAIRS * P, q=P)
        x1T = sb("x1T", [P, KC, P])
        y, z, x1, res = fw_a[:, 0, :], fw_a[:, 1, :], fw_b[:, 0, :], fw_b[:, 1, :]
        ssk = sb("ssk", [P, NT + 1])
        ssq = sb("ssq", [P, HEADS])
        mc, mm, cm, es, sc, dc, rc = (sb(n, [P, HEADS]) for n in ("mc", "mm", "cm", "es", "sc", "dc", "rc"))
        dn, dn2, dn3, r8 = (sb(n, [P, PAIRS]) for n in ("dn", "dn2", "dn3", "r8"))
        bns, mv = sb("bns", [P, 6]), sb("mv", [P, 2])
        nx, ny, nu = sb("nx", [P, NT + 1]), sb("ny", [P, NT + 1]), sb("nu", [P, NT + 1])

        PS = ctx.enter_context(nc.psum_tensor("PS", [P, 8 * 512], f32))

        def bank(b, n=1):
            return PS[:, 512 * b:512 * (b + n)]

        s_h = [sem(f"s_h{g}") for g in range(4)]
        s_tab, s_w, s_comp, s_wg, s_wo, s_small = (sem(n) for n in ("s_tab", "s_w", "s_comp", "s_wg", "s_wo", "s_small"))
        s_id, s_idb = sem("s_id"), sem("s_idb")
        s_ps = sem("s_ps")
        s_eva, s_evd = sem("s_eva"), sem("s_evd")
        s_kn, s_fw, s_fs, s_e, s_sm = (sem(n) for n in ("s_kn", "s_fw", "s_fs", "s_e", "s_sm"))
        s_setp, s_sets, s_setd = sem("s_setp"), sem("s_sets"), sem("s_setd")
        p_q, p_sw, p_cs, p_o, p_qt, p_pv, p_ct, p_at, p_xt, p_f = (sem(n) for n in (
            "p_q", "p_sw", "p_cs", "p_o", "p_qt", "p_pv", "p_ct", "p_at", "p_xt", "p_f"))
        a_sq, a_tanh, a_es, a_ec, a_ecs, a_qt, a_ct, a_at, a_xt, a_xc, a_kw = (sem(n) for n in (
            "a_sq", "a_tanh", "a_es", "a_ec", "a_ecs", "a_qt", "a_ct", "a_at", "a_xt", "a_xc", "a_kw"))
        d_red, d_qs, d_rope, d_csub, d_cm, d_rc, d_ao, d_x1, d_fr, d_out = (sem(n) for n in (
            "d_red", "d_qs", "d_rope", "d_csub", "d_cm", "d_rc", "d_ao", "d_x1", "d_fr", "d_out"))
        g_mask, g_rope, g_cn = sem("g_mask"), sem("g_rope"), sem("g_cn")
        s_out, s_chain = sem("s_out"), sem("s_chain")

        def wait(eng, s, value):
            if not isinstance(value, int) or value > 0:
                eng.wait_ge(s, value)

        G_H, G_XC, G_K, G_V, G_CR, G_CK, G_WG, G_WE, G_KT, G_CKT, G_CW, G_FS, G_FT, G_END = np.cumsum(
            [0, 8, 4, 4, 8, 1, 1, 8, 8, 4, 1, 8, 1, 1]).tolist()

        def ours(mine, start, n):
            return [g for g in range(n) if (start + g) % 2 == mine]

        def two(g):
            return bank(g % 8).rearrange("p (k n) -> p k n", k=2)

        def four(g):
            return bank(g % 8).rearrange("p (t d) -> p t d", d=D)

        def copied(eng, g):
            if g >= 0:
                eng.wait_ge(s_evd if g % 2 else s_eva, g // 2 + 1)

        def all_steps(body, eng):
            body(-1, True, False, False)
            body(0, True, True, False)
            with eng.Fori(1, NT - 1) as i:
                body(i, True, True, True)
            body(NT - 1, False, True, True)
            body(NT, False, False, True)

        block_ctx = ctx.enter_context(nc.Block())

        @block_ctx.sync
        def _(sp):
            for g in range(4):
                sp.dma_start(H[:, 4 * g:4 * g + 4, :], h_v[:, 4 * g:4 * g + 4, :]).then_inc(s_h[g], 16)
            sp.dma_start(wcomp_s[:, :, :], wcomp.rearrange("(m p) d -> p m d", p=P)).then_inc(s_comp, 16)
            sp.dma_start(wg_s[:, :, :], wg.rearrange("g (f p) i -> p (g f) i", p=P)).then_inc(s_wg, 16)
            sp.dma_start(rope_s[:, :, :], rope_t).then_inc(s_tab, 16)
            sp.dma_start(block_f[:, :, :], block_t).then_inc(s_tab, 16)
            sp.dma_start(window_s[:, :, :], window_t).then_inc(s_tab, 16)
            sp.wait_ge(d_out, 1)
            sp.dma_start(out_v[0:P, :], res[:, :]).then_inc(s_out, 16)
            with sp.Fori(1, NT) as i:
                row = sp.snap(i * P)
                sp.wait_ge(d_out, i + 1)
                sp.dma_start(out_v[ds(row, P), :], res[:, :]).then_inc(s_out, 16)
            sp.wait_ge(s_out, 16 * NT + 16)

        @block_ctx.tensor
        def _(pe):
            group = [0]

            def begin():
                g = group[0]
                copied(pe, g - 8)
                return bank(g % 8)

            def end(ins):
                ins.then_inc(s_ps, 1)
                group[0] += 1

            pe.wait_ge(s_id, 2)
            for g in range(8):
                pe.wait_ge(s_h[g // 2], 16)
                b = begin()
                for k in range(KC):
                    for t in range(2):
                        last = nc.tensor.transpose(b[:, (2 * k + t) * P:(2 * k + t + 1) * P],
                                                   H[:, 2 * g + t, k * P:(k + 1) * P], ident[:, :])
                end(last)
            pe.wait_ge(s_w, 64)
            for g in range(4):
                copied(pe, 2 * g)
                copied(pe, 2 * g + 1)
                b = begin()
                at = WIN + (g % 2) * 512
                for k in range(KC):
                    last = nc.tensor.matmul(b[0:QC, :], wqc_s[:, k, :], hT[:, k, g // 2, at:at + 512],
                                            start=k == 0, stop=k == KC - 1)
                end(last)
            for g in range(4):
                b = begin()
                for t in range(4 * g, 4 * g + 4):
                    at = WIN + (t % TPB) * P
                    for k in range(KC):
                        last = nc.tensor.matmul(b[:, (t % 4) * D:(t % 4 + 1) * D], hT[:, k, t // TPB, at:at + P],
                                                wk_s[:, k, :], start=k == 0, stop=k == KC - 1)
                end(last)
            for g in range(8):
                b = begin()
                for w in range(4 * g, 4 * g + 4):
                    at = (w % (2 * TPB)) * WIN
                    for k in range(KC):
                        last = nc.tensor.matmul(b[:, (w % 4) * D:(w % 4 + 1) * D],
                                                hT[:, k, w // (2 * TPB), at:at + P],
                                                wv_s[:, k, :], start=k == 0, stop=k == KC - 1)
                end(last)
            b = begin()
            pe.wait_ge(s_comp, 16)
            for m in range(BLK):
                for k in range(KC):
                    rows = hT[:, k, :, WIN:].rearrange("p b (n m) -> p b n m", m=BLK)[:, :, :, m]
                    last = nc.tensor.matmul(b[:, 0:P], wcomp_s[:, KC * m + k, :], rows,
                                            start=m == k == 0, stop=m == BLK - 1 and k == KC - 1)
            end(last)
            copied(pe, G_CR)
            b = begin()
            end(nc.tensor.transpose(b[:, 0:D], ckr[:, :], ident[:, :]))
            pe.wait_ge(s_wg, 16)
            for g in range(8):
                b = begin()
                for k in range(KC):
                    for f in range(2):
                        last = nc.tensor.transpose(b[:, (2 * k + f) * P:(2 * k + f + 1) * P],
                                                   wg_s[:, 2 * g + f, k * P:(k + 1) * P], ident[:, :])
                end(last)
            pe.wait_ge(s_wo, 16)
            for g in range(8):
                copied(pe, G_WG + g)
                b = begin()
                for f in range(2):
                    hd = 2 * g + f
                    for k in range(KC):
                        last = nc.tensor.matmul(b[:, f * HID:(f + 1) * HID], wgT[:, k, hd * P:(hd + 1) * P],
                                                wo_s[:, (hd // GROUPS) * KC + k, :], start=k == 0, stop=k == KC - 1)
                end(last)
            pe.wait_ge(s_kn, 1)
            for g in range(4):
                b = begin()
                for t in range(4):
                    last = nc.tensor.transpose(b[:, t * P:(t + 1) * P], K[:, 4 * g + t, :], ident[:, :])
                end(last)
            b = begin()
            end(nc.tensor.transpose(b[:, 0:P], K[:, NT, :], ident[:, :]))
            pe.wait_ge(s_setd, 1)
            copied(pe, G_WE + 6)
            copied(pe, G_WE + 7)
            for g in range(8):
                b = begin()
                for f in range(2):
                    bt, pr = g // 4, 2 * (g % 4) + f
                    for par in range(2):
                        last = nc.tensor.matmul(b[par * 64:par * 64 + 64, f * HID:(f + 1) * HID],
                                                ckTv[:, bt, :], Weff[:, 2 * pr + par, :], start=True, stop=True)
                end(last)
            pe.wait_ge(s_fs, 1)
            b = begin()
            end(nc.tensor.matmul(b[:, 0:1], ones[:, :], fsum[:, :], start=True, stop=True))
            pe.wait_ge(s_fw, 1)
            b = begin()
            for k in range(KC):
                for o in range(KC):
                    last = nc.tensor.transpose(b[:, (2 * k + o) * P:(2 * k + o + 1) * P],
                                               fw_s[:, o, k * P:(k + 1) * P], ident[:, :])
            end(last)
            for g in range(G_END - 8, G_END):
                copied(pe, g)
            pe.wait_ge(s_sets, 1)
            pe.wait_ge(s_setd, 2)

            def step(i, front, mid, back):
                if front:
                    pe.wait_ge(a_xc, i + 2)
                    if isinstance(i, int):
                        wait(pe, a_qt, 2 * i + 2)
                    for hf in range(2):
                        wait(pe, *((a_ct, 2 * i - 1) if hf else (a_at, 2 * i)))
                        for c in range(2):
                            n = 2 * hf + c
                            last = nc.tensor.matmul(bank(n), xcF[:, :], wqup_s[:, n * 512:(n + 1) * 512],
                                                    start=True, stop=True)
                        last.then_inc(p_q, 1)
                if mid:
                    pe.wait_ge(a_kw, i + 1)
                    pe.wait_ge(a_qt, 2 * i + 2)
                    for u, b in enumerate((4, 5, 6, 4)):
                        wait(pe, *((a_at, 2 * i - 1), (a_at, 2 * i - 1), (a_ct, 2 * i), (a_tanh, 4 * i + 1))[u])
                        c, hf = divmod(u, 2)
                        nc.tensor.matmul(bank(b), kTw[:, c * WIN:c * WIN + P],
                                         qT[:, 8 * hf:8 * hf + 8, c * WIN:(c + 1) * WIN],
                                         start=True, stop=True).then_inc(p_sw, 1)
                    pe.wait_ge(a_tanh, 4 * i + 3)
                    bt = i // TPB
                    maskrow = block_b[:, ds(i % TPB, 1), :].to_broadcast([P, 8, NBLK])
                    for hf in range(2):
                        nc.tensor.matmul(bank(5 + hf), identb[:, :], maskrow, start=True, stop=True)
                        for hd in range(8):
                            last = nc.tensor.matmul(bank(5 + hf)[:, hd * NBLK:(hd + 1) * NBLK], qT[:, 8 * hf + hd, :],
                                                    ckTs[:, ds(bt, 1), :], start=False, stop=True,
                                                    skip_group_check=True)
                    last.then_inc(p_cs, 1)
                if back:
                    t = i - 1
                    pe.wait_ge(a_at, 2 * t + 2)
                    pe.wait_ge(a_ct, 2 * t + 2)
                    pe.wait_ge(d_fr, t + 1)
                    o = bank(7)[:, 0:HID]
                    for hd in range(HEADS):
                        nc.tensor.matmul(o, aoT[:, hd // 2, hd % 2, :, :].rearrange("p c q -> p (c q)"), Weff[:, hd, :],
                                         start=hd == 0, stop=False)
                    bt = t // TPB
                    for pr in range(PAIRS):
                        last = nc.tensor.matmul(o, PcT[:, pr, :], CW[:, ds(bt, 1), pr, :],
                                                start=False, stop=pr == PAIRS - 1)
                    last.then_inc(p_o, 1)
                if front:
                    pe.wait_ge(g_rope, i + 2)
                    pe.wait_ge(d_qs, 2 * i + 4)
                    for hf in range(2):
                        for hd in range(8):
                            last = nc.tensor.transpose(bank(2 * hf, 2)[:, hd * P:(hd + 1) * P],
                                                       qs[:, 8 * hf + hd, :], ident[:, :])
                        last.then_inc(p_qt, 1)
                if mid:
                    for c in range(2):
                        pe.wait_ge(g_mask, 2 * i + c + 1)
                        if c == 0:
                            pe.wait_ge(a_tanh, 4 * i + 4)
                            pe.wait_ge(d_csub, i + 1)
                        elif front:
                            pe.wait_ge(a_qt, 2 * i + 4)
                        for pr in range(PAIRS):
                            o = bank((4, 0)[c] + pr // 3)[:, (pr % 3) * VW:(pr % 3 + 1) * VW]
                            last = nc.tensor.matmul(o, Pm[:, c, 2 * pr:2 * pr + 2, :], V[:, ds(2 * i + c, 1), 0:VW],
                                                    start=True, stop=True)
                        last.then_inc(p_pv, 1)
                    pe.wait_ge(g_cn, i + 1)
                    for pr in range(4):
                        last = nc.tensor.transpose(bank(3)[:, pr * P:(pr + 1) * P], Pn[:, 2 * pr:2 * pr + 2, :],
                                                   ident[:, :])
                    last.then_inc(p_ct, 1)
                    pe.wait_ge(d_ao, 2 * i + 1)
                    for pr in range(PAIRS):
                        last = nc.tensor.transpose(bank(4, 2)[:, pr * P:(pr + 1) * P], ao[:, 0, pr, :], ident[:, :])
                    last.then_inc(p_at, 1)
                    for pr in range(4, 8):
                        last = nc.tensor.transpose(bank(6)[:, (pr - 4) * P:(pr - 3) * P],
                                                   Pn[:, 2 * pr:2 * pr + 2, :], ident[:, :])
                    last.then_inc(p_ct, 1)
                if back:
                    t = i - 1
                    pe.wait_ge(d_x1, t + 1)
                    for k in range(KC):
                        last = nc.tensor.transpose(bank(7)[:, k * P:(k + 1) * P], x1[:, k * P:(k + 1) * P], ident[:, :])
                    last.then_inc(p_xt, 1)
                if mid:
                    pe.wait_ge(d_ao, 2 * i + 2)
                    for pr in range(PAIRS):
                        last = nc.tensor.transpose(bank(0, 2)[:, pr * P:(pr + 1) * P], ao[:, 1, pr, :], ident[:, :])
                    last.then_inc(p_at, 1)
                if back:
                    pe.wait_ge(a_xt, t + 1)
                    for k in range(KC):
                        last = nc.tensor.matmul(bank(7)[:, HID:2 * HID], x1T[:, k, :], wfT[:, k, :],
                                                start=k == 0, stop=k == KC - 1)
                    last.then_inc(p_f, 1)

            all_steps(step, pe)

        @block_ctx.scalar
        def _(act):
            act.dma_start(wqc_s[:, :, :], wqc.rearrange("(k p) n -> p k n", p=P)).then_inc(s_w, 16)
            act.dma_start(wk_s[:, :, :], wk.rearrange("(k p) n -> p k n", p=P)).then_inc(s_w, 16)
            act.dma_start(wv_s[:, :, :], wv.rearrange("(k p) n -> p k n", p=P)).then_inc(s_w, 16)
            act.dma_start(wqup_s[:, :], wqup).then_inc(s_w, 16)
            act.dma_start(wo_s[:, :, :], wo.rearrange("(k p) n -> p k n", p=P)).then_inc(s_wo, 16)
            act.dma_start(fw_s[:, :, :], fw.rearrange("(k p) n -> p k n", p=P)).then_inc(s_small, 16)
            act.dma_start(qw[:, :], qnw.rearrange("(p a) -> p a", a=1)).then_inc(s_small, 16)
            act.dma_start(kw[:, :], knw.rearrange("(p a) -> p a", a=1)).then_inc(s_small, 16)
            act.dma_start(sinkb[:, :], sink.partition_broadcast(P)).then_inc(s_small, 16)
            act.dma_start(fb_s[:, :], fb.partition_broadcast(P)).then_inc(s_small, 16)

            def evac(g, dst, src, scale=1.0):
                act.wait_ge(s_ps, g + 1)
                nc.scalar.mul(dst, src, scale).then_inc(s_eva, 1)

            act.wait_ge(s_idb, 1)
            for g in ours(0, G_H, 8):
                at = WIN + (g % 4) * 256
                evac(g, hT[:, :, g // 4, at:at + 256], two(g))
            for g in ours(0, G_XC, 4):
                evac(G_XC + g, xcT[:, g * 512:(g + 1) * 512], bank((G_XC + g) % 8)[0:QC, :])
            for g in ours(0, G_K, 4):
                evac(G_K + g, K[:, 4 * g:4 * g + 4, :], four(G_K + g))
            for g in ours(0, G_V, 8):
                evac(G_V + g, V[:, 4 * g:4 * g + 4, 0:D], four(G_V + g))
            if G_CR % 2 == 0:
                evac(G_CR, ckr[:, :], bank(G_CR % 8)[:, 0:P])
            if G_CK % 2 == 0:
                evac(G_CK, K[:, NT, :], bank(G_CK % 8)[:, 0:D])
            for g in ours(0, G_WG, 8):
                evac(G_WG + g, wgT[:, :, 2 * g * P:2 * g * P + 256], two(G_WG + g))
            for g in ours(0, G_WE, 8):
                evac(G_WE + g, Weff[:, 2 * g:2 * g + 2, :], two(G_WE + g))
            act.wait_ge(s_sm, 1)
            nc.scalar.activation(e0[:, :], skm[:, :], ACT.Exp, scale=-1.0).then_inc(s_e, 1)
            nc.scalar.activation(e1[:, :], skp[:, :], ACT.Exp).then_inc(s_e, 1)
            nc.scalar.activation(block_b[:, :, :], block_f[:, :, :], ACT.Copy).then_inc(s_sets, 1)
            for g in ours(0, G_KT, 4):
                at = WIN + (g % 2) * 512
                evac(G_KT + g, kT[:, g // 2, at:at + 512], bank((G_KT + g) % 8), wqk[:, 0:1])
            if G_CKT % 2 == 0:
                act.wait_ge(s_setd, 1)
                evac(G_CKT, ckTs[:, :, :], bank(G_CKT % 8)[:, 0:P].rearrange("p (b n) -> p b n", b=BATCH), wqk[:, 0:1])
            for g in ours(0, G_CW, 8):
                evac(G_CW + g, CW[:, g // 4, 2 * (g % 4):2 * (g % 4) + 2, :], two(G_CW + g))
            if G_FS % 2 == 0:
                evac(G_FS, fscale[:, :], bank(G_FS % 8)[:, 0:1], 1.0 / (HID * HID))
            if G_FT % 2 == 0:
                evac(G_FT, wfT[:, :, :], two(G_FT))
            copied(act, G_XC + 3)
            copied(act, G_KT)
            copied(act, G_KT + 1)
            act.wait_ge(s_eva, (G_END + 1) // 2)

            def narrow(dst, src, s):
                nc.scalar.activation(dst, src, ACT.Copy).then_inc(s, 1)

            def step(i, front, mid, back):
                if front:
                    if isinstance(i, int) and i == -1:
                        narrow(xcF[:, :], xcT[:, 0:P], a_xc)
                        narrow(kTw[:, :], kT[:, 0, 0:P + WIN], a_kw)
                    for hf in range(2):
                        act.wait_ge(p_q, 2 * i + 3 + hf)
                        wait(act, d_red, 2 * i + 2)
                        nc.scalar.activation(sq[:, 8 * hf:8 * hf + 8, :],
                                             bank(2 * hf, 2).rearrange("p (a d) -> p a d", d=D),
                                             ACT.Square).then_inc(a_sq, 1)
                if mid:
                    for u, b in enumerate((4, 5, 6, 4)):
                        c, hf = divmod(u, 2)
                        wait(act, a_es, 2 * i)
                        act.wait_ge(p_sw, 4 * i + u + 1)
                        nc.scalar.activation(th[:, c, 8 * hf:8 * hf + 8, :], bank(b).rearrange("p (a q) -> p a q", q=WIN),
                                             ACT.Tanh, scale=1.0 / CAP).then_inc(a_tanh, 1)
                    for c in range(2):
                        wait(act, g_mask, 2 * i + c - 1)
                        act.wait_ge(a_tanh, 4 * i + 2 * c + 2)
                        nc.scalar.activation(E[:, c, :, :], th[:, c, :, :], ACT.Exp, scale=CAP).then_inc(a_es, 1)
                if front:
                    act.wait_ge(p_q, 2 * i + 4)
                    narrow(xcF[:, :], xcT[:, ds((i + 2) * P, P)], a_xc)
                    if mid:
                        act.wait_ge(p_sw, 4 * i + 4)
                        at = (i + 1) * P + ((i + 1) // TPB) * WIN
                        narrow(kTw[:, :], kT[:, :, :].rearrange("p b s -> p (b s)")[:, ds(at, P + WIN)], a_kw)
                if mid:
                    act.wait_ge(d_csub, i + 1)
                    wait(act, g_cn, i)
                    nc.scalar.activation(Ec[:, :, :], Cs[:, :, :], ACT.Exp).then_inc(a_ec, 1)
                    act.wait_ge(d_cm, i + 1)
                    nc.scalar.activation(es[:, :], cm[:, :], ACT.Exp).then_inc(a_ecs, 1)
                if front:
                    for hf in range(2):
                        act.wait_ge(p_qt, 2 * i + 3 + hf)
                        narrow(qT[:, 8 * hf:8 * hf + 8, :], bank(2 * hf, 2).rearrange("p (a q) -> p a q", q=P), a_qt)
                if mid:
                    act.wait_ge(p_ct, 2 * i + 1)
                    narrow(PcT[:, 0:4, :], bank(3).rearrange("p (a q) -> p a q", q=P), a_ct)
                    act.wait_ge(p_at, 2 * i + 1)
                    narrow(aoT[:, :, :, 0, :], bank(4, 2).rearrange("p (a r q) -> p a r q", r=2, q=WIN), a_at)
                    act.wait_ge(p_ct, 2 * i + 2)
                    narrow(PcT[:, 4:8, :], bank(6).rearrange("p (a q) -> p a q", q=P), a_ct)
                if back:
                    act.wait_ge(p_xt, i)
                    narrow(x1T[:, :, :], bank(7)[:, 0:HID].rearrange("p (k n) -> p k n", k=KC), a_xt)
                if mid:
                    act.wait_ge(p_at, 2 * i + 2)
                    narrow(aoT[:, :, :, 1, :], bank(0, 2).rearrange("p (a r q) -> p a r q", r=2, q=WIN), a_at)

            all_steps(step, act)

        @block_ctx.vector
        def _(dve):
            V_ = nc.vector
            base, since = [0], [0]

            def link(ins):
                ins.then_inc(s_chain, 1)
                since[0] += 1
                dve.wait_ge(s_chain, base[0] + since[0])

            def rsqrt(x, yv, uv):
                link(V_.tensor_single_scalar(uv.bitcast(i32), x.bitcast(i32), 1, ALU.logical_shift_right))
                link(V_.tensor_scalar(yv.bitcast(i32), uv.bitcast(i32), -1.0, float(0x5F3759DF), ALU.mult, ALU.add))
                for _ in range(3):
                    link(V_.tensor_tensor(uv, x, yv, ALU.mult))
                    link(V_.scalar_tensor_tensor(uv, uv, -0.5, yv, ALU.mult, ALU.mult))
                    link(V_.scalar_tensor_tensor(yv, uv, 1.5, yv, ALU.add, ALU.mult))

            def evac(g, dst, src, scale=None):
                dve.wait_ge(s_ps, g + 1)
                if scale is None:
                    V_.tensor_copy(dst, src).then_inc(s_evd, 1)
                else:
                    V_.tensor_scalar(dst, src, scale, None, ALU.mult).then_inc(s_evd, 1)

            V_.memset(ones[:, :], 1.0).then_inc(s_id, 1)
            V_.memset(V[:, :, D:VS], 1.0)
            V_.memset(xcT[:, NT * P:], 0.0)
            dve.wait_ge(s_idb, 1)
            for g in ours(1, G_H, 8):
                at = WIN + (g % 4) * 256
                evac(g, hT[:, :, g // 4, at:at + 256], two(g))
            for g in ours(1, G_XC, 4):
                evac(G_XC + g, xcT[:, g * 512:(g + 1) * 512], bank((G_XC + g) % 8)[0:QC, :])
            for g in ours(1, G_K, 4):
                evac(G_K + g, K[:, 4 * g:4 * g + 4, :], four(G_K + g))
            dve.wait_ge(s_small, 80)
            link(V_.scalar_tensor_tensor(wqk[:, :], qw[:, :], SCALE, kw[:, :], ALU.mult, ALU.mult))
            for par in range(2):
                rows = slice(par * 64, par * 64 + 64)
                sk = sinkb[rows, :].rearrange("p (a r) -> p r a", r=2)[:, par, :]
                V_.tensor_scalar(skm[rows, :], sk, 0.0, None, ALU.max)
                link(V_.tensor_copy(dn[rows, :], sk))
            link(V_.tensor_tensor(skp[:, :], dn[:, :], skm[:, :], ALU.subtract))
            V_.tensor_reduce(fsum[:, :], fw_s[:, :, :], AX.XY, ALU.add, apply_absolute_value=True).then_inc(s_fs, 1)
            V_.tensor_copy(skp[:, 0:1], skp[:, 0:1]).then_inc(s_sm, 1)
            for g in ours(1, G_V, 8):
                evac(G_V + g, V[:, 4 * g:4 * g + 4, 0:D], four(G_V + g))
            if G_CR % 2 == 1:
                evac(G_CR, ckr[:, :], bank(G_CR % 8)[:, 0:P])
            if G_CK % 2 == 1:
                evac(G_CK, K[:, NT, :], bank(G_CK % 8)[:, 0:D])
            copied(dve, G_K + 2)
            copied(dve, G_K + 3)
            copied(dve, G_CK)
            link(V_.tensor_tensor(sqk, K[:, 0:NT, :], K[:, 0:NT, :], ALU.mult))
            link(V_.tensor_reduce(ssk[:, 0:NT], sqk, AX.X, ALU.add))
            link(V_.tensor_tensor(sqk[:, 0, :], K[:, NT, :], K[:, NT, :], ALU.mult))
            link(V_.tensor_reduce(ssk[:, NT:], sqk[:, 0:1, :], AX.X, ALU.add))
            link(V_.tensor_scalar(nx[:, :], ssk[:, :], 1.0 / D, 1e-6, ALU.mult, ALU.add))
            rsqrt(nx[:, :], ny[:, :], nu[:, :])
            link(V_.tensor_tensor(K[:, :, :], K[:, :, :], ny[:, :].unsqueeze(2).to_broadcast([P, NT + 1, D]), ALU.mult))
            dve.wait_ge(s_tab, 48)
            for bt in range(BATCH):
                t = slice(bt * TPB, bt * TPB + TPB)
                V_.tensor_tensor(rt1[:, t, :], K[:, t, 0:ROPE], rope_s[:, :, 0:ROPE], ALU.mult)
                V_.tensor_tensor(rt2[:, t, 0:32], K[:, t, 32:64], rope_s[:, :, 64:96], ALU.mult)
                link(V_.tensor_tensor(rt2[:, t, 32:64], K[:, t, 0:32], rope_s[:, :, 96:128], ALU.mult))
            V_.tensor_tensor(K[:, 0:NT, 0:ROPE], rt1[:, :, :], rt2[:, :, :], ALU.add).then_inc(s_kn, 1)
            for g in ours(1, G_WG, 8):
                evac(G_WG + g, wgT[:, :, 2 * g * P:2 * g * P + 256], two(G_WG + g))
            for g in ours(1, G_WE, 8):
                evac(G_WE + g, Weff[:, 2 * g:2 * g + 2, :], two(G_WE + g))
            for g in ours(1, G_KT, 4):
                at = WIN + (g % 2) * 512
                evac(G_KT + g, kT[:, g // 2, at:at + 512], bank((G_KT + g) % 8), wqk[:, 0:1])
            dve.wait_ge(s_ps, G_CKT + 1)
            ckb = bank(G_CKT % 8)[:, 0:P].rearrange("p (b n) -> p b n", b=BATCH)
            V_.tensor_scalar(ckTv[:, :, :], ckb, kw[:, 0:1], None, ALU.mult).then_inc(s_setd, 1)
            if G_CKT % 2 == 1:
                evac(G_CKT, ckTs[:, :, :], ckb, wqk[:, 0:1])
            for g in ours(1, G_CW, 8):
                evac(G_CW + g, CW[:, g // 4, 2 * (g % 4):2 * (g % 4) + 2, :], two(G_CW + g))
            if G_FS % 2 == 1:
                evac(G_FS, fscale[:, :], bank(G_FS % 8)[:, 0:1], 1.0 / (HID * HID))
            copied(dve, G_FS)
            link(V_.tensor_scalar(fthr[:, :], fscale[:, :], 1e-10, 0.5, ALU.add, ALU.mult))
            link(V_.tensor_scalar(fthn[:, :], fthr[:, :], -1.0, None, ALU.mult))
            V_.tensor_scalar(fw_a[:, :, :], fw_s[:, :, :], fthr[:, 0:1], fscale[:, 0:1], ALU.is_gt, ALU.mult)
            link(V_.tensor_scalar(fw_b[:, :, :], fw_s[:, :, :], fthn[:, 0:1], fscale[:, 0:1], ALU.is_lt, ALU.mult))
            V_.tensor_tensor(fw_s[:, :, :], fw_a[:, :, :], fw_b[:, :, :], ALU.subtract).then_inc(s_fw, 1)
            if G_FT % 2 == 1:
                evac(G_FT, wfT[:, :, :], two(G_FT))
            dve.wait_ge(s_evd, G_END // 2)
            dve.wait_ge(s_e, 2)
            V_.memset(nu[:, :], 1.0).then_inc(d_fr, 1)
            V_.memset(nx[:, :], 1.0).then_inc(s_out, 16)
            V_.memset(ny[:, :], 1.0).then_inc(s_setd, 1)
            base[0], since[0] = since[0], 0

            def layernorm(src, dst):
                link(V_.bn_stats(bns[:, :], src[:, :]))
                V_.memset(nu[:, 0:1], 0.0)
                link(V_.bn_aggr(mv[:, :], bns[:, :]))
                link(V_.tensor_scalar(nx[:, 0:1], mv[:, 1:2], 1e-5, None, ALU.add))
                rsqrt(nx[:, 0:1], ny[:, 0:1], nu[:, 0:1])
                return V_.tensor_scalar(dst[:, :], src[:, :], mv[:, 0:1], ny[:, 0:1], ALU.subtract, ALU.mult)

            def step(i, front, mid, back):
                if front:
                    t = i + 1
                    for hf in range(2):
                        dve.wait_ge(a_sq, 2 * t + hf + 1)
                        V_.tensor_reduce(ssq[:, 8 * hf:8 * hf + 8], sq[:, 8 * hf:8 * hf + 8, :], AX.X, ALU.add).then_inc(d_red, 1)
                    dve.wait_ge(d_red, 2 * t + 2)
                    link(V_.tensor_scalar(nx[:, 0:HEADS], ssq[:, :], 1.0 / D, 1e-6, ALU.mult, ALU.add))
                    rsqrt(nx[:, 0:HEADS], ny[:, 0:HEADS], nu[:, 0:HEADS])
                    wait(dve, p_qt, 2 * t)
                    for hf in range(2):
                        heads = slice(8 * hf, 8 * hf + 8)
                        V_.tensor_tensor(qs[:, heads, :], bank(2 * hf, 2).rearrange("p (a d) -> p a d", d=D),
                                         ny[:, heads].unsqueeze(2).to_broadcast([P, 8, D]), ALU.mult).then_inc(d_qs, 1)
                    dve.wait_ge(d_qs, 2 * t + 2)
                    wait(dve, g_rope, t)
                    tab = rope_s[:, ds(t % TPB, 1), :]
                    V_.tensor_tensor(rt1[:, :, :], qs[:, :, 0:ROPE], tab[:, :, 0:64].to_broadcast([P, HEADS, 64]), ALU.mult)
                    V_.tensor_tensor(rt2[:, :, 0:32], qs[:, :, 32:64], tab[:, :, 64:96].to_broadcast([P, HEADS, 32]), ALU.mult)
                    V_.tensor_tensor(rt2[:, :, 32:64], qs[:, :, 0:32], tab[:, :, 96:128].to_broadcast([P, HEADS, 32]),
                                     ALU.mult).then_inc(d_rope, 1)
                if mid:
                    S = bank(5, 2).rearrange("p (a n) -> p a n", n=NBLK)
                    dve.wait_ge(p_cs, i + 1)
                    link(V_.tensor_reduce(mc[:, :], S, AX.X, ALU.max))
                    link(V_.tensor_tensor(mm[:, :], mc[:, :], sinkb[:, :], ALU.max))
                    wait(dve, a_ec, i)
                    V_.tensor_tensor(Cs[:, :, :], S, mm[:, :].unsqueeze(2).to_broadcast([P, HEADS, NBLK]),
                                     ALU.subtract).then_inc(d_csub, 1)
                    wait(dve, a_ecs, i)
                    V_.tensor_tensor(cm[:, :], sinkb[:, :], mm[:, :], ALU.subtract).then_inc(d_cm, 1)
                    dve.wait_ge(a_ec, i + 1)
                    link(V_.tensor_reduce(sc[:, :], Ec[:, :, :], AX.X, ALU.add))
                    dve.wait_ge(a_ecs, i + 1)
                    link(V_.tensor_tensor(dc[:, :], sc[:, :], es[:, :], ALU.add))
                    wait(dve, g_cn, i)
                    V_.reciprocal(rc[:, :], dc[:, :]).then_inc(d_rc, 1)
                if back:
                    t = i - 1
                    dve.wait_ge(p_o, t + 1)
                    link(V_.tensor_tensor(y[:, :], bank(7)[:, 0:HID], H[:, ds(t, 1), :].rearrange("p a n -> p (a n)"), ALU.add))
                    layernorm(y, x1).then_inc(d_x1, 1)
                if mid:
                    for c in range(2):
                        dve.wait_ge(p_pv, 2 * i + c + 1)
                        parts = []
                        for kb, n in enumerate((3, 3, 2)):
                            parts.append((slice(3 * kb, 3 * kb + n), n,
                                          bank((4, 0)[c] + kb)[:, 0:n * VW].rearrange("p (a d) -> p a d", d=VW)))
                        for pairs, n, pv in parts:
                            last = V_.tensor_tensor(dn[:, pairs], pv[:, :, D], e0[:, pairs], ALU.mult)
                        link(last)
                        link(V_.tensor_tensor(dn2[:, :], dn[:, :], e1[:, :], ALU.add))
                        link(V_.reciprocal(dn3[:, :], dn2[:, :]))
                        link(V_.tensor_tensor(r8[:, :], dn3[:, :], e0[:, :], ALU.mult))
                        wait(dve, p_at, 2 * i + c - 1)
                        for pairs, n, pv in parts:
                            last = V_.tensor_tensor(ao[:, c, pairs, :], pv[:, :, 0:D],
                                                    r8[:, pairs].unsqueeze(2).to_broadcast([P, n, D]), ALU.mult)
                        last.then_inc(d_ao, 1)
                        dve.wait_ge(d_ao, 2 * i + c + 1)
                if back:
                    dve.wait_ge(p_f, t + 1)
                    link(V_.tensor_tensor(y[:, :], bank(7)[:, HID:2 * HID], x1[:, :], ALU.add))
                    V_.tensor_tensor(z[:, :], y[:, :], fb_s[:, :], ALU.add).then_inc(d_fr, 1)
                    dve.wait_ge(d_fr, t + 2)
                    dve.wait_ge(s_out, 16 * t + 16)
                    layernorm(z, res).then_inc(d_out, 1)

            body_links = {}

            def counted(i, front, mid, back):
                if isinstance(i, int):
                    step(i, front, mid, back)
                    base[0], since[0] = base[0] + since[0], 0
                    return
                before = base[0]
                base[0] = before + (i - 1) * LINKS
                step(i, front, mid, back)
                assert since[0] == LINKS, since[0]
                base[0], since[0] = before + (NT - 2) * LINKS, 0

            LINKS = 1 + 11 + 2 + 2 + 1 + 3 + 11 + 8 + 1 + 3 + 11
            all_steps(counted, dve)

        @block_ctx.gpsimd
        def _(pool):
            G = nc.gpsimd
            G.memset(ident[:, :], 0.0).then_inc(s_setp, 1)
            for k in range(KC):
                for bt in range(BATCH):
                    last = G.memset(hT[:, k, bt, 0:WIN], 0.0)
            last.then_inc(s_idb, 1)
            G.memset(kT[:, :, 0:WIN], 0.0).then_inc(s_setp, 1)
            pool.wait_ge(s_setp, 2)
            G.affine_select(out=ident[:, :], in_=ident[:, :], compare_op=ALU.not_equal, fill=1.0,
                            base=0, pattern=[[-1, P]], channel_multiplier=1).then_inc(s_id, 1)
            pool.wait_ge(s_id, 2)
            G.tensor_copy(identb[:, :], ident[:, :]).then_inc(s_setp, 1)
            pool.wait_ge(s_tab, 48)

            def step(i, front, mid, back):
                if mid:
                    for c in range(2):
                        pool.wait_ge(a_es, 2 * i + c + 1)
                        wait(pool, p_pv, 2 * i + c - 1)
                        mask = window_s[:, 1:2, :] if c else window_s[:, ds(i % TPB, 1), :]
                        G.tensor_tensor(Pm[:, c, :, :], E[:, c, :, :], mask.to_broadcast([P, HEADS, WIN]),
                                        ALU.mult).then_inc(g_mask, 1)
                if front:
                    pool.wait_ge(d_rope, i + 2)
                    G.tensor_tensor(qs[:, :, 0:ROPE], rt1[:, :, :], rt2[:, :, :], ALU.add).then_inc(g_rope, 1)
                if mid:
                    pool.wait_ge(d_rc, i + 1)
                    wait(pool, p_ct, 2 * i)
                    G.tensor_tensor(Pn[:, :, :], Ec[:, :, :], rc[:, :].unsqueeze(2).to_broadcast([P, HEADS, NBLK]),
                                    ALU.mult).then_inc(g_cn, 1)

            all_steps(step, pool)


_INS = ["L0_attn_h", "L0_attn_Wq_c", "L0_attn_Wq_up", "L0_attn_Wk", "L0_attn_Wv", "L0_attn_W_comp",
        "L0_attn_q_norm_w", "L0_attn_k_norm_w", "L0_attn_sink", "L0_attn_Wg", "L0_attn_Wo",
        "L0_ffn_weight", "L0_ffn_bias"]


def kernel(**inputs):
    import numpy as _np
    import concourse.bacc as _bacc
    from concourse import mybir as _mybir
    from concourse.bass_utils import run_bass_kernel_spmd as _run

    nc = _bacc.Bacc("TRN2", target_bir_lowering=False, num_devices=1)
    arrays = {f"in_{n}": _np.ascontiguousarray(inputs[n]) for n in _INS}
    for name, table in zip(("rope", "block", "window"), shape_tables()):
        arrays[f"table_{name}"] = table
    args = [nc.dram_tensor(n, a.shape, _mybir.dt.from_np(a.dtype), kind="ExternalInput").ap()
            for n, a in arrays.items()]
    out = nc.dram_tensor("out", (BATCH, SEQ, HID), _mybir.dt.float32, kind="ExternalOutput").ap()
    build(nc, *args, out)
    return _run(nc, [arrays], core_ids=[0]).results[0]["out"]
```

```python
from contextlib import ExitStack

import concourse.bass as bass
import numpy as np
from concourse import mybir

BATCH, SEQ, HID = 2, 1024, 256
HEADS, D, QC = 16, 128, 64
BLK, WIN = 16, 64
ROPE = 64
GROUPS, INTER = 4, 256
CAP = 50.0
P = 128
NT = BATCH * SEQ // P
TPB = SEQ // P
NBLK = SEQ // BLK
PAIRS = HEADS // 2
KC = HID // P
VW = D + 1
VS = D + 2
SPAN = WIN + SEQ
SCALE = float(D) ** -0.5
TAB = 2 * ROPE
MASKED = -1e30


def shape_tables():
    inv = np.float32(1.0) / np.float32(10000.0) ** (np.arange(0, ROPE, 2, dtype=np.float32) / np.float32(ROPE))
    ang = np.arange(SEQ, dtype=np.float32)[:, None] * inv[None, :].astype(np.float32)
    cos, sin = np.cos(ang), np.sin(ang)
    rope = np.concatenate([cos, cos, -sin, sin], 1).astype(np.float32)
    rope = rope.reshape(TPB, P, TAB).transpose(1, 0, 2).copy()
    t = np.arange(SEQ)
    end = np.arange(NBLK) * BLK + BLK - 1
    block = np.where(end[None] < t[:, None], 0.0, MASKED).astype(np.float32)
    block = block.reshape(TPB, P, NBLK).transpose(1, 0, 2).copy()
    p, q = np.arange(P)[:, None], np.arange(WIN)[None]
    usual = ((p > q) & (p <= q + WIN)).astype(np.float32)
    first = usual * (p >= WIN)
    window = np.stack([first] + [usual] * (TPB - 1), 1).astype(np.float32)
    return rope, block, np.ascontiguousarray(window)


def build(nc, h, wqc, wqup, wk, wv, wcomp, qnw, knw, sink, wg, wo, fw, fb, rope_t, block_t, window_t, out):
    f32, bf16, i32 = mybir.dt.float32, mybir.dt.bfloat16, mybir.dt.int32
    f32r, f16 = mybir.dt.float32r, mybir.dt.float16
    ALU, ACT, AX = mybir.AluOpType, mybir.ActivationFunctionType, mybir.AxisListType
    ds = bass.ds

    h_v = h.rearrange("b (j p) c -> p (b j) c", p=P)
    out_v = out.rearrange("b s c -> (b s) c")

    ctx = ExitStack()
    with ctx:
        def sb(name, shape, dt=f32):
            return ctx.enter_context(nc.sbuf_tensor(name, shape, dt))

        def sem(name):
            return ctx.enter_context(nc.semaphore(name))

        H = sb("H", [P, NT, HID])
        ident, identb = sb("ident", [P, P]), sb("identb", [P, P], bf16)
        ones = sb("ones", [P, P])
        rope_s = sb("rope_s", [P, TPB, TAB])
        block_f, block_b = sb("block_f", [P, TPB, NBLK]), sb("block_b", [P, TPB, NBLK], bf16)
        window_s = sb("window_s", [P, TPB, WIN])
        wqup_p = sb("wqup_p", [P, 2, HEADS * D], f32r)
        xcT = sb("xcT", [P, (NT + 1) * P], f32r)
        kT = sb("kT", [P, 2, BATCH * SPAN], f16)
        V = sb("V", [P, 2 * NT, VS])
        ckTs = sb("ckTs", [P, 2, BATCH * NBLK], f16)
        ckTv = sb("ckTv", [P, BATCH, NBLK])
        Weff = sb("Weff", [P, HEADS, HID])
        CW = sb("CW", [P, BATCH, PAIRS, HID])
        wfT = sb("wfT", [P, KC, HID])
        fb_s = sb("fb_s", [P, HID])
        sinkb, sinkr = sb("sinkb", [P, HEADS]), sb("sinkr", [P, HEADS])
        e0, e1, skp, skm = (sb(n, [P, PAIRS]) for n in ("e0", "e1", "skp", "skm"))
        qw, kw, wqk = (sb(n, [P, 1]) for n in ("qw", "kw", "wqk"))

        room_h, room_comp, room_wg, room_wgT = (sb(n, [P, w]) for n, w in (
            ("room_h", KC * BATCH * SPAN), ("room_comp", BLK * KC * D),
            ("room_wg", HEADS * INTER), ("room_wgT", KC * HEADS * P)))
        hT = room_h[:, :].rearrange("p (k b s) -> p k b s", k=KC, b=BATCH)
        wcomp_s = room_comp[:, :].rearrange("p (m d) -> p m d", d=D)
        wg_s = room_wg[:, :].rearrange("p (f i) -> p f i", i=INTER)
        wgT = room_wgT[:, :].rearrange("p (k f) -> p k f", k=KC)
        wqc_s, wk_s, wv_s = sb("wqc_s", [P, KC, QC]), sb("wk_s", [P, KC, D]), sb("wv_s", [P, KC, D])
        room_wo, room_K = sb("room_wo", [P, GROUPS * KC * HID]), sb("room_K", [P, (NT + 1) * D])
        wo_s = room_wo[:, :].rearrange("p (k n) -> p k n", n=HID)
        K = room_K[:, :].rearrange("p (t d) -> p t d", d=D)
        fw_s, fw_a, fw_b = (sb(n, [P, KC, HID]) for n in ("fw_s", "fw_a", "fw_b"))
        ckr = sb("ckr", [P, P])
        fsum, fscale, fthr, fthn = (sb(n, [P, 1]) for n in ("fsum", "fscale", "fthr", "fthn"))

        def part(room, start, pattern, size=HEADS * D, **axes):
            return room[:, start:start + size].rearrange(pattern, **axes)

        sq = part(room_K, 0, "p (a d) -> p a d", d=D)
        sqk = part(room_comp, 0, "p (a d) -> p a d", d=D)
        rt1 = part(room_comp, 2048, "p (a d) -> p a d", HEADS * ROPE, d=ROPE)
        rt2 = part(room_comp, 3072, "p (a d) -> p a d", HEADS * ROPE, d=ROPE)
        wqup_s = CW[:, 0, :, :].rearrange("p a n -> p (a n)")
        xcF = sb("xcF", [P, P], f32r)
        kTw = sb("kTw", [P, 2, P + WIN], f16)
        E = part(room_comp, 0, "p (c a q) -> p c a q", c=2, q=WIN)
        Pm = part(room_wg, 0, "p (c a q) -> p c a q", c=2, q=WIN)
        ao = part(room_wg, 2048, "p (c a d) -> p c a d", c=2, d=D)
        aoT = part(room_wgT, 0, "p (a r c q) -> p a r c q", c=2, r=2, q=WIN)
        qs = part(room_wgT, 2048, "p (a d) -> p a d", d=D)
        qT = part(room_h, 0, "p (h a q) -> p h a q", h=2, q=P // 2).bitcast(f16)
        Ec = part(room_h, 3072, "p (a n) -> p a n", HEADS * NBLK, n=NBLK)
        Pn = part(room_wo, 0, "p (a n) -> p a n", HEADS * NBLK, n=NBLK)
        PcT = part(room_wo, 1024, "p (a q) -> p a q", PAIRS * P, q=P)
        x1T = sb("x1T", [P, KC, P])
        y, z, x1, res = fw_a[:, 0, :], fw_a[:, 1, :], fw_b[:, 0, :], fw_b[:, 1, :]
        ssk = sb("ssk", [P, NT + 1])
        ssq = sb("ssq", [P, HEADS])
        mc, mm, mn, cm, es, sc, dc, rc = (sb(n, [P, HEADS]) for n in ("mc", "mm", "mn", "cm", "es", "sc", "dc", "rc"))
        spare = sb("spare", [P, 1])
        dn, dn2, dn3, r8 = (sb(n, [P, PAIRS]) for n in ("dn", "dn2", "dn3", "r8"))
        bns, mv = sb("bns", [P, 2, 6]), sb("mv", [P, 2, 2])
        nx, ny, nu = sb("nx", [P, NT + 2]), sb("ny", [P, NT + 2]), sb("nu", [P, NT + 2])

        PS = ctx.enter_context(nc.psum_tensor("PS", [P, 8 * 512], f32))

        def bank(b, n=1):
            return PS[:, 512 * b:512 * (b + n)]

        s_h = [sem(f"s_h{g}") for g in range(4)]
        s_tab, s_w, s_comp, s_wg, s_wo, s_small = (sem(n) for n in ("s_tab", "s_w", "s_comp", "s_wg", "s_wo", "s_small"))
        s_id, s_idb = sem("s_id"), sem("s_idb")
        s_ps = sem("s_ps")
        s_eva, s_evd = sem("s_eva"), sem("s_evd")
        s_hi, s_lo = sem("s_hi"), sem("s_lo")
        s_kn, s_fw, s_fs, s_e, s_sm = (sem(n) for n in ("s_kn", "s_fw", "s_fs", "s_e", "s_sm"))
        s_setp, s_sets, s_setd = sem("s_setp"), sem("s_sets"), sem("s_setd")
        p_q, p_sw, p_cs, p_o, p_qt, p_pv, p_ct, p_at, p_xt, p_f = (sem(n) for n in (
            "p_q", "p_sw", "p_cs", "p_o", "p_qt", "p_pv", "p_ct", "p_at", "p_xt", "p_f"))
        a_sq, a_tanh, a_es, a_ec, a_ecs, a_qt, a_ct, a_at, a_xt, a_xc, a_kw = (sem(n) for n in (
            "a_sq", "a_tanh", "a_es", "a_ec", "a_ecs", "a_qt", "a_ct", "a_at", "a_xt", "a_xc", "a_kw"))
        s_wq, d_ql = sem("s_wq"), sem("d_ql")
        d_red, d_qs, d_rope, d_cmax, d_cm, d_rc, d_ao, d_x1, d_fr, d_y, d_out = (sem(n) for n in (
            "d_red", "d_qs", "d_rope", "d_cmax", "d_cm", "d_rc", "d_ao", "d_x1", "d_fr", "d_y", "d_out"))
        g_mask, g_rope, g_cn, g_rt = (sem(n) for n in ("g_mask", "g_rope", "g_cn", "g_rt"))
        s_out, s_chain = sem("s_out"), sem("s_chain")

        def qbank(hf):
            return bank(2 - 2 * hf, 2)

        def wait(eng, s, value):
            if not isinstance(value, int) or value > 0:
                eng.wait_ge(s, value)

        G_H, G_XC, G_K, G_V, G_CR, G_CK, G_WG, G_WE, G_KT, G_CKT, G_CW, G_FS, G_FT, G_END = np.cumsum(
            [0, 8, 4, 4, 8, 1, 1, 8, 8, 4, 1, 8, 1, 1]).tolist()

        def ours(mine, start, n):
            return [g for g in range(n) if (start + g) % 2 == mine]

        def two(g):
            return bank(g % 8).rearrange("p (k n) -> p k n", k=2)

        def four(g):
            return bank(g % 8).rearrange("p (t d) -> p t d", d=D)

        def key_parts(g):
            if g == 4:
                return ckTs[:, 0, :], bank(G_CKT % 8)[:, 0:P], ckTs[:, 1, :]
            at = (g // 2) * SPAN + WIN + (g % 2) * 512
            return kT[:, 0, at:at + 512], bank((G_KT + g) % 8), kT[:, 1, at:at + 512]

        def copied(eng, g):
            if g < 0:
                return
            for first, n, at in ((G_XC, 4, 1), (G_KT, 5, 5)):
                if first <= g < first + n:
                    eng.wait_ge(s_lo, at + g - first + 1)
                    return
            plain = [x for x in range(g + 1) if not (G_XC <= x < G_XC + 4 or G_KT <= x < G_KT + 5)]
            eng.wait_ge(s_evd if g % 2 else s_eva, sum(x % 2 == g % 2 for x in plain))

        PARTS = ((0, 0), (1, 0), (0, 1))

        def all_steps(body, eng):
            def at(i):
                body(i, *(0 <= i + 1 - n < NT for n in range(5)))

            for i in range(-1, 3):
                at(i)
            with eng.Fori(3, NT - 1) as i:
                body(i, *[True] * 5)
            for i in range(NT - 1, NT + 3):
                at(i)

        block_ctx = ctx.enter_context(nc.Block())

        @block_ctx.sync
        def _(sp):
            for g in range(4):
                sp.dma_start(H[:, 4 * g:4 * g + 4, :], h_v[:, 4 * g:4 * g + 4, :]).then_inc(s_h[g], 16)
            sp.dma_start(wcomp_s[:, :, :], wcomp.rearrange("(m p) d -> p m d", p=P)).then_inc(s_comp, 16)
            sp.dma_start(wg_s[:, :, :], wg.rearrange("g (f p) i -> p (g f) i", p=P)).then_inc(s_wg, 16)
            sp.dma_start(rope_s[:, :, :], rope_t).then_inc(s_tab, 16)
            sp.dma_start(block_f[:, :, :], block_t).then_inc(s_tab, 16)
            sp.dma_start(window_s[:, :, :], window_t).then_inc(s_tab, 16)
            sp.wait_ge(d_out, 1)
            sp.dma_start(out_v[0:P, :], res[:, :]).then_inc(s_out, 16)
            with sp.Fori(1, NT) as i:
                row = sp.snap(i * P)
                sp.wait_ge(d_out, i + 1)
                sp.dma_start(out_v[ds(row, P), :], res[:, :]).then_inc(s_out, 16)
            sp.wait_ge(s_out, 16 * NT + 16)

        @block_ctx.tensor
        def _(pe):
            group = [0]

            def begin():
                g = group[0]
                copied(pe, g - 8)
                return bank(g % 8)

            def end(ins):
                ins.then_inc(s_ps, 1)
                group[0] += 1

            pe.wait_ge(s_id, 2)
            for g in range(8):
                pe.wait_ge(s_h[g // 2], 16)
                b = begin()
                for k in range(KC):
                    for t in range(2):
                        last = nc.tensor.transpose(b[:, (2 * k + t) * P:(2 * k + t + 1) * P],
                                                   H[:, 2 * g + t, k * P:(k + 1) * P], ident[:, :])
                end(last)
            pe.wait_ge(s_w, 48)
            for g in range(4):
                copied(pe, 2 * g)
                copied(pe, 2 * g + 1)
                b = begin()
                at = WIN + (g % 2) * 512
                for k in range(KC):
                    last = nc.tensor.matmul(b[0:QC, :], wqc_s[:, k, :], hT[:, k, g // 2, at:at + 512],
                                            start=k == 0, stop=k == KC - 1)
                end(last)
            for g in range(4):
                b = begin()
                for t in range(4 * g, 4 * g + 4):
                    at = WIN + (t % TPB) * P
                    for k in range(KC):
                        last = nc.tensor.matmul(b[:, (t % 4) * D:(t % 4 + 1) * D], hT[:, k, t // TPB, at:at + P],
                                                wk_s[:, k, :], start=k == 0, stop=k == KC - 1)
                end(last)
            for g in range(8):
                b = begin()
                for w in range(4 * g, 4 * g + 4):
                    at = (w % (2 * TPB)) * WIN
                    for k in range(KC):
                        last = nc.tensor.matmul(b[:, (w % 4) * D:(w % 4 + 1) * D],
                                                hT[:, k, w // (2 * TPB), at:at + P],
                                                wv_s[:, k, :], start=k == 0, stop=k == KC - 1)
                end(last)
            b = begin()
            pe.wait_ge(s_comp, 16)
            for m in range(BLK):
                for k in range(KC):
                    rows = hT[:, k, :, WIN:].rearrange("p b (n m) -> p b n m", m=BLK)[:, :, :, m]
                    last = nc.tensor.matmul(b[:, 0:P], wcomp_s[:, KC * m + k, :], rows,
                                            start=m == k == 0, stop=m == BLK - 1 and k == KC - 1)
            end(last)
            copied(pe, G_CR)
            b = begin()
            end(nc.tensor.transpose(b[:, 0:D], ckr[:, :], ident[:, :]))
            pe.wait_ge(s_wg, 16)
            for g in range(8):
                b = begin()
                for k in range(KC):
                    for f in range(2):
                        last = nc.tensor.transpose(b[:, (2 * k + f) * P:(2 * k + f + 1) * P],
                                                   wg_s[:, 2 * g + f, k * P:(k + 1) * P], ident[:, :])
                end(last)
            pe.wait_ge(s_wo, 16)
            for g in range(8):
                copied(pe, G_WG + g)
                b = begin()
                for f in range(2):
                    hd = 2 * g + f
                    for k in range(KC):
                        last = nc.tensor.matmul(b[:, f * HID:(f + 1) * HID], wgT[:, k, hd * P:(hd + 1) * P],
                                                wo_s[:, (hd // GROUPS) * KC + k, :], start=k == 0, stop=k == KC - 1)
                end(last)
            pe.wait_ge(s_kn, 1)
            for g in range(4):
                b = begin()
                for t in range(4):
                    last = nc.tensor.transpose(b[:, t * P:(t + 1) * P], K[:, 4 * g + t, :], ident[:, :])
                end(last)
            b = begin()
            end(nc.tensor.transpose(b[:, 0:P], K[:, NT, :], ident[:, :]))
            pe.wait_ge(s_setd, 1)
            copied(pe, G_WE + 6)
            copied(pe, G_WE + 7)
            for g in range(8):
                b = begin()
                for f in range(2):
                    bt, pr = g // 4, 2 * (g % 4) + f
                    for par in range(2):
                        last = nc.tensor.matmul(b[par * 64:par * 64 + 64, f * HID:(f + 1) * HID],
                                                ckTv[:, bt, :], Weff[:, 2 * pr + par, :], start=True, stop=True)
                end(last)
            pe.wait_ge(s_fs, 1)
            b = begin()
            end(nc.tensor.matmul(b[:, 0:1], ones[:, :], fsum[:, :], start=True, stop=True))
            pe.wait_ge(s_fw, 1)
            b = begin()
            for k in range(KC):
                for o in range(KC):
                    last = nc.tensor.transpose(b[:, (2 * k + o) * P:(2 * k + o + 1) * P],
                                               fw_s[:, o, k * P:(k + 1) * P], ident[:, :])
            end(last)
            for g in range(G_END - 8, G_END):
                copied(pe, g)
            pe.wait_ge(s_sets, 1)
            pe.wait_ge(s_setd, 2)

            def step(i, front, mid, proj, ffn, last_norm):
                if front:
                    pe.wait_ge(a_xc, i + 2)
                    if isinstance(i, int):
                        wait(pe, d_ql, 2 * i + 2)
                    for hf in range(2):
                        wait(pe, *((a_at, 2 * i) if hf else (a_ct, 2 * i - 1)))
                        for n in (2 * hf, 2 * hf + 1):
                            for w in range(2):
                                last = nc.tensor.matmul(qbank(hf)[:, (n % 2) * 512:(n % 2 + 1) * 512], xcF[:, :], wqup_p[:, w, n * 512:(n + 1) * 512],
                                                        start=w == 0, stop=w == 1)
                        last.then_inc(p_q, 1)
                if mid:
                    pe.wait_ge(a_kw, i + 1)
                    pe.wait_ge(d_ql, 2 * i + 2)
                    for u, b in enumerate((4, 5, 6, 4)):
                        wait(pe, *((a_at, 2 * i - 1), (a_at, 2 * i - 1), (a_ct, 2 * i), (a_tanh, 4 * i + 1))[u])
                        c, hf = divmod(u, 2)
                        for n, (kp, qp) in enumerate(PARTS):
                            last = nc.tensor.matmul(bank(b), kTw[:, kp, c * WIN:c * WIN + P],
                                                    qT[:, qp, 8 * hf:8 * hf + 8, c * WIN:(c + 1) * WIN],
                                                    start=n == 0, stop=n == 2)
                        last.then_inc(p_sw, 1)
                    pe.wait_ge(a_tanh, 4 * i + 3)
                    blocks = (i // TPB) * NBLK
                    maskrow = block_b[:, ds(i % TPB, 1), :].to_broadcast([P, 8, NBLK])
                    for hf in range(2):
                        nc.tensor.matmul(bank(5 + hf), identb[:, :], maskrow, start=True, stop=True)
                        for hd in range(8):
                            for kp, qp in PARTS:
                                last = nc.tensor.matmul(bank(5 + hf)[:, hd * NBLK:(hd + 1) * NBLK],
                                                        qT[:, qp, 8 * hf + hd, :], ckTs[:, kp, ds(blocks, NBLK)],
                                                        start=False, stop=True, skip_group_check=True)
                    last.then_inc(p_cs, 1)
                o = bank(7)[:, 0:HID]
                if proj:
                    t = i - 1
                    pe.wait_ge(a_at, 2 * t + 2)
                    wait(pe, d_y, t)
                    wait(pe, d_fr, t - 1)
                    for hd in range(HEADS):
                        nc.tensor.matmul(o, aoT[:, hd // 2, hd % 2, :, :].rearrange("p c q -> p (c q)"), Weff[:, hd, :],
                                         start=hd == 0, stop=False)

                def values(c):
                    pe.wait_ge(g_mask, 2 * i + c + 1)
                    if c == 0:
                        pe.wait_ge(a_tanh, 4 * i + 4)
                        pe.wait_ge(a_ec, i + 1)
                    elif front:
                        pe.wait_ge(d_ql, 2 * i + 4)
                    for pr in range(PAIRS):
                        pv = bank((4, 0)[c] + pr // 3)[:, (pr % 3) * VW:(pr % 3 + 1) * VW]
                        last = nc.tensor.matmul(pv, Pm[:, c, 2 * pr:2 * pr + 2, :], V[:, ds(2 * i + c, 1), 0:VW],
                                                start=True, stop=True)
                    last.then_inc(p_pv, 1)

                if mid:
                    values(0)
                if front:
                    for hf in range(2):
                        pe.wait_ge(g_rope, 2 * i + 3 + hf)
                        pe.wait_ge(d_qs, 2 * i + 3 + hf)
                        for hd in range(8):
                            last = nc.tensor.transpose(qbank(hf)[:, hd * P:(hd + 1) * P],
                                                       qs[:, 8 * hf + hd, :], ident[:, :])
                        last.then_inc(p_qt, 1)
                if proj:
                    pe.wait_ge(a_ct, 2 * t + 2)
                    bt = t // TPB
                    for pr in range(PAIRS):
                        last = nc.tensor.matmul(o, PcT[:, pr, :], CW[:, ds(bt, 1), pr, :],
                                                start=False, stop=pr == PAIRS - 1)
                    last.then_inc(p_o, 1)
                if mid:
                    values(1)
                if ffn:
                    pe.wait_ge(d_x1, i - 1)
                    wait(pe, d_fr, i - 2)
                    wait(pe, d_y, i if proj else NT)
                    for k in range(KC):
                        last = nc.tensor.transpose(bank(7)[:, HID + k * P:HID + (k + 1) * P],
                                                   x1[:, k * P:(k + 1) * P], ident[:, :])
                    last.then_inc(p_xt, 1)
                if mid:
                    pe.wait_ge(g_cn, i + 1)
                    for pr in range(4):
                        last = nc.tensor.transpose(bank(3)[:, pr * P:(pr + 1) * P], Pn[:, 2 * pr:2 * pr + 2, :],
                                                   ident[:, :])
                    last.then_inc(p_ct, 1)
                    pe.wait_ge(d_ao, 2 * i + 1)
                    for pr in range(PAIRS):
                        last = nc.tensor.transpose(bank(4, 2)[:, pr * P:(pr + 1) * P], ao[:, 0, pr, :], ident[:, :])
                    last.then_inc(p_at, 1)
                if ffn:
                    pe.wait_ge(a_xt, i - 1)
                    for k in range(KC):
                        last = nc.tensor.matmul(bank(7)[:, HID:2 * HID], x1T[:, k, :], wfT[:, k, :],
                                                start=k == 0, stop=k == KC - 1)
                    last.then_inc(p_f, 1)
                if mid:
                    for pr in range(4, 8):
                        last = nc.tensor.transpose(bank(6)[:, (pr - 4) * P:(pr - 3) * P],
                                                   Pn[:, 2 * pr:2 * pr + 2, :], ident[:, :])
                    last.then_inc(p_ct, 1)
                    pe.wait_ge(d_ao, 2 * i + 2)
                    for pr in range(PAIRS):
                        last = nc.tensor.transpose(bank(0, 2)[:, pr * P:(pr + 1) * P], ao[:, 1, pr, :], ident[:, :])
                    last.then_inc(p_at, 1)

            all_steps(step, pe)

        @block_ctx.scalar
        def _(act):
            act.dma_start(wqc_s[:, :, :], wqc.rearrange("(k p) n -> p k n", p=P)).then_inc(s_w, 16)
            act.dma_start(wk_s[:, :, :], wk.rearrange("(k p) n -> p k n", p=P)).then_inc(s_w, 16)
            act.dma_start(wv_s[:, :, :], wv.rearrange("(k p) n -> p k n", p=P)).then_inc(s_w, 16)
            for r in range(2):
                act.dma_start(wqup_s[r * QC:(r + 1) * QC, :], wqup).then_inc(s_wq, 16)
            act.dma_start(wo_s[:, :, :], wo.rearrange("(k p) n -> p k n", p=P)).then_inc(s_wo, 16)
            act.dma_start(fw_s[:, :, :], fw.rearrange("(k p) n -> p k n", p=P)).then_inc(s_small, 16)
            act.dma_start(qw[:, :], qnw.rearrange("(p a) -> p a", a=1)).then_inc(s_small, 16)
            act.dma_start(kw[:, :], knw.rearrange("(p a) -> p a", a=1)).then_inc(s_small, 16)
            act.dma_start(sinkb[:, :], sink.partition_broadcast(P)).then_inc(s_small, 16)
            act.dma_start(fb_s[:, :], fb.partition_broadcast(P)).then_inc(s_small, 16)

            def evac(g, dst, src, scale=1.0):
                act.wait_ge(s_ps, g + 1)
                nc.scalar.mul(dst, src, scale).then_inc(s_eva, 1)

            act.wait_ge(s_idb, 1)
            for g in ours(0, G_H, 8):
                at = WIN + (g % 4) * 256
                evac(g, hT[:, :, g // 4, at:at + 256], two(g))
            act.wait_ge(s_wq, 32)
            nc.scalar.activation(wqup_p[:, 0, :], wqup_s[:, :], ACT.Copy).then_inc(s_hi, 1)
            for g in range(4):
                act.wait_ge(s_ps, G_XC + g + 1)
                nc.scalar.activation(xcT[0:QC, g * 512:(g + 1) * 512], bank((G_XC + g) % 8)[0:QC, :],
                                     ACT.Copy).then_inc(s_hi, 1)
            for g in ours(0, G_K, 4):
                evac(G_K + g, K[:, 4 * g:4 * g + 4, :], four(G_K + g))
            for g in ours(0, G_V, 8):
                evac(G_V + g, V[:, 4 * g:4 * g + 4, 0:D], four(G_V + g))
            if G_CR % 2 == 0:
                evac(G_CR, ckr[:, :], bank(G_CR % 8)[:, 0:P])
            if G_CK % 2 == 0:
                evac(G_CK, K[:, NT, :], bank(G_CK % 8)[:, 0:D])
            for g in ours(0, G_WG, 8):
                evac(G_WG + g, wgT[:, :, 2 * g * P:2 * g * P + 256], two(G_WG + g))
            for g in ours(0, G_WE, 8):
                evac(G_WE + g, Weff[:, 2 * g:2 * g + 2, :], two(G_WE + g))
            act.wait_ge(s_sm, 1)
            nc.scalar.activation(e0[:, :], skm[:, :], ACT.Exp, scale=-1.0).then_inc(s_e, 1)
            nc.scalar.activation(e1[:, :], skp[:, :], ACT.Exp).then_inc(s_e, 1)
            nc.scalar.activation(block_b[:, :, :], block_f[:, :, :], ACT.Copy).then_inc(s_sets, 1)
            for g in range(5):
                act.wait_ge(s_ps, G_KT + g + 1)
                if g == 4:
                    act.wait_ge(s_setd, 1)
                nc.scalar.mul(*key_parts(g)[:2], wqk[:, 0:1]).then_inc(s_hi, 1)
            for g in ours(0, G_CW, 8):
                evac(G_CW + g, CW[:, g // 4, 2 * (g % 4):2 * (g % 4) + 2, :], two(G_CW + g))
            if G_FS % 2 == 0:
                evac(G_FS, fscale[:, :], bank(G_FS % 8)[:, 0:1], 1.0 / (HID * HID))
            if G_FT % 2 == 0:
                evac(G_FT, wfT[:, :, :], two(G_FT))
            copied(act, G_CKT)
            copied(act, G_END - 1)
            copied(act, G_END - 2)

            def narrow(dst, src, s):
                nc.scalar.activation(dst, src, ACT.Copy).then_inc(s, 1)

            def step(i, front, mid, proj, ffn, last_norm):
                if front:
                    if isinstance(i, int) and i == -1:
                        narrow(xcF[:, :], xcT[:, 0:P].bitcast(f32), a_xc)
                        narrow(kTw[:, :, :], kT[:, :, 0:P + WIN], a_kw)
                    for hf in range(2):
                        act.wait_ge(p_q, 2 * i + 3 + hf)
                        wait(act, d_red, 2 * i + 2)
                        nc.scalar.activation(sq[:, 8 * hf:8 * hf + 8, :],
                                             qbank(hf).rearrange("p (a d) -> p a d", d=D),
                                             ACT.Square).then_inc(a_sq, 1)
                if mid:
                    for u, b in enumerate((4, 5, 6, 4)):
                        c, hf = divmod(u, 2)
                        if hf == 0:
                            wait(act, g_mask, 2 * i + c - 1)
                        act.wait_ge(p_sw, 4 * i + u + 1)
                        nc.scalar.activation(E[:, c, 8 * hf:8 * hf + 8, :], bank(b).rearrange("p (a q) -> p a q", q=WIN),
                                             ACT.Tanh, scale=SCALE / CAP).then_inc(a_tanh, 1)
                    for c in range(2):
                        act.wait_ge(a_tanh, 4 * i + 2 * c + 2)
                        nc.scalar.activation(E[:, c, :, :], E[:, c, :, :], ACT.Exp, scale=CAP).then_inc(a_es, 1)
                if front:
                    act.wait_ge(p_q, 2 * i + 4)
                    narrow(xcF[:, :], xcT[:, ds((i + 2) * P, P)].bitcast(f32), a_xc)
                    if mid:
                        act.wait_ge(p_sw, 4 * i + 4)
                        at = (i + 1) * P + ((i + 1) // TPB) * WIN
                        narrow(kTw[:, :, :], kT[:, :, ds(at, P + WIN)], a_kw)
                if mid:
                    act.wait_ge(d_cmax, i + 1)
                    wait(act, g_cn, i)
                    for hd in range(HEADS):
                        last = nc.scalar.activation(Ec[:, hd, :], bank(5, 2)[:, hd * NBLK:(hd + 1) * NBLK], ACT.Exp,
                                                    scale=SCALE, bias=mn[:, hd:hd + 1], accum_out=sc[:, hd:hd + 1])
                    last.then_inc(a_ec, 1)
                    act.wait_ge(d_cm, i + 1)
                    nc.scalar.activation(es[:, :], cm[:, :], ACT.Exp).then_inc(a_ecs, 1)
                if front:
                    for hf in range(2):
                        act.wait_ge(p_qt, 2 * i + 3 + hf)
                        narrow(qT[:, 0, 8 * hf:8 * hf + 8, :], qbank(hf).rearrange("p (a q) -> p a q", q=P), a_qt)
                if ffn:
                    act.wait_ge(p_xt, i - 1)
                    narrow(x1T[:, :, :], bank(7)[:, HID:2 * HID].rearrange("p (k n) -> p k n", k=KC), a_xt)
                if mid:
                    act.wait_ge(p_ct, 2 * i + 1)
                    narrow(PcT[:, 0:4, :], bank(3).rearrange("p (a q) -> p a q", q=P), a_ct)
                    act.wait_ge(p_at, 2 * i + 1)
                    narrow(aoT[:, :, :, 0, :], bank(4, 2).rearrange("p (a r q) -> p a r q", r=2, q=WIN), a_at)
                    act.wait_ge(p_ct, 2 * i + 2)
                    narrow(PcT[:, 4:8, :], bank(6).rearrange("p (a q) -> p a q", q=P), a_ct)
                    act.wait_ge(p_at, 2 * i + 2)
                    narrow(aoT[:, :, :, 1, :], bank(0, 2).rearrange("p (a r q) -> p a r q", r=2, q=WIN), a_at)

            all_steps(step, act)

        @block_ctx.vector
        def _(dve):
            V_ = nc.vector
            base, since = [0], [0]

            def link(ins):
                ins.then_inc(s_chain, 1)
                since[0] += 1
                dve.wait_ge(s_chain, base[0] + since[0])

            def after_link():
                dve.wait_ge(s_chain, base[0] + since[0])

            def chained(ins):
                ins.then_inc(s_chain, 1)
                since[0] += 1

            def rsqrt_part(n, x, yv, uv):
                after_link()
                if n == 0:
                    chained(V_.tensor_single_scalar(uv.bitcast(i32), x.bitcast(i32), 1, ALU.logical_shift_right))
                elif n == 1:
                    chained(V_.tensor_scalar(yv.bitcast(i32), uv.bitcast(i32), -1.0, float(0x5F3759DF), ALU.mult, ALU.add))
                elif n % 3 == 2:
                    chained(V_.tensor_tensor(uv, x, yv, ALU.mult))
                elif n % 3 == 0:
                    chained(V_.scalar_tensor_tensor(uv, uv, -0.5, yv, ALU.mult, ALU.mult))
                else:
                    chained(V_.scalar_tensor_tensor(yv, uv, 1.5, yv, ALU.add, ALU.mult))

            def rsqrt(x, yv, uv):
                for n in range(11):
                    rsqrt_part(n, x, yv, uv)
                after_link()

            def evac(g, dst, src, scale=None):
                dve.wait_ge(s_ps, g + 1)
                if scale is None:
                    V_.tensor_copy(dst, src).then_inc(s_evd, 1)
                else:
                    V_.tensor_scalar(dst, src, scale, None, ALU.mult).then_inc(s_evd, 1)

            V_.memset(ones[:, :], 1.0).then_inc(s_id, 1)
            V_.memset(V[:, :, D:VS], 1.0)
            V_.memset(xcT[:, NT * P:].bitcast(f32), 0.0)
            dve.wait_ge(s_idb, 1)
            for g in ours(1, G_H, 8):
                at = WIN + (g % 4) * 256
                evac(g, hT[:, :, g // 4, at:at + 256], two(g))
            dve.wait_ge(s_hi, 1)
            V_.tensor_tensor(wqup_p[:, 1, :], wqup_s[:, :], wqup_p[:, 0, :].bitcast(f32), ALU.subtract).then_inc(s_lo, 1)
            for g in range(4):
                dve.wait_ge(s_hi, g + 2)
                V_.tensor_tensor(xcT[QC:P, g * 512:(g + 1) * 512], bank((G_XC + g) % 8)[0:QC, :],
                                 xcT[0:QC, g * 512:(g + 1) * 512].bitcast(f32), ALU.subtract).then_inc(s_lo, 1)
            for g in ours(1, G_K, 4):
                evac(G_K + g, K[:, 4 * g:4 * g + 4, :], four(G_K + g))
            dve.wait_ge(s_small, 80)
            link(V_.tensor_tensor(wqk[:, :], qw[:, :], kw[:, :], ALU.mult))
            for par in range(2):
                rows = slice(par * 64, par * 64 + 64)
                sk = sinkb[rows, :].rearrange("p (a r) -> p r a", r=2)[:, par, :]
                V_.tensor_scalar(skm[rows, :], sk, 0.0, None, ALU.max)
                link(V_.tensor_copy(dn[rows, :], sk))
            link(V_.tensor_tensor(skp[:, :], dn[:, :], skm[:, :], ALU.subtract))
            V_.tensor_reduce(fsum[:, :], fw_s[:, :, :], AX.XY, ALU.add, apply_absolute_value=True).then_inc(s_fs, 1)
            V_.tensor_copy(skp[:, 0:1], skp[:, 0:1]).then_inc(s_sm, 1)
            for g in ours(1, G_V, 8):
                evac(G_V + g, V[:, 4 * g:4 * g + 4, 0:D], four(G_V + g))
            if G_CR % 2 == 1:
                evac(G_CR, ckr[:, :], bank(G_CR % 8)[:, 0:P])
            if G_CK % 2 == 1:
                evac(G_CK, K[:, NT, :], bank(G_CK % 8)[:, 0:D])
            copied(dve, G_K + 2)
            copied(dve, G_K + 3)
            copied(dve, G_CK)
            link(V_.tensor_tensor(sqk, K[:, 0:NT, :], K[:, 0:NT, :], ALU.mult))
            link(V_.tensor_reduce(ssk[:, 0:NT], sqk, AX.X, ALU.add))
            link(V_.tensor_tensor(sqk[:, 0, :], K[:, NT, :], K[:, NT, :], ALU.mult))
            link(V_.tensor_reduce(ssk[:, NT:], sqk[:, 0:1, :], AX.X, ALU.add))
            link(V_.tensor_scalar(nx[:, 0:NT + 1], ssk[:, :], 1.0 / D, 1e-6, ALU.mult, ALU.add))
            rsqrt(nx[:, 0:NT + 1], ny[:, 0:NT + 1], nu[:, 0:NT + 1])
            link(V_.tensor_scalar(sinkr[:, :], sinkb[:, :], 1.0 / SCALE, None, ALU.mult))
            link(V_.tensor_tensor(K[:, :, :], K[:, :, :], ny[:, 0:NT + 1].unsqueeze(2).to_broadcast([P, NT + 1, D]), ALU.mult))
            dve.wait_ge(s_tab, 48)
            for bt in range(BATCH):
                t = slice(bt * TPB, bt * TPB + TPB)
                V_.tensor_tensor(rt1[:, t, :], K[:, t, 0:ROPE], rope_s[:, :, 0:ROPE], ALU.mult)
                V_.tensor_tensor(rt2[:, t, 0:32], K[:, t, 32:64], rope_s[:, :, 64:96], ALU.mult)
                link(V_.tensor_tensor(rt2[:, t, 32:64], K[:, t, 0:32], rope_s[:, :, 96:128], ALU.mult))
            V_.tensor_tensor(K[:, 0:NT, 0:ROPE], rt1[:, :, :], rt2[:, :, :], ALU.add).then_inc(s_kn, 1)
            for g in ours(1, G_WG, 8):
                evac(G_WG + g, wgT[:, :, 2 * g * P:2 * g * P + 256], two(G_WG + g))
            for g in ours(1, G_WE, 8):
                evac(G_WE + g, Weff[:, 2 * g:2 * g + 2, :], two(G_WE + g))
            for g in range(4):
                dve.wait_ge(s_hi, 6 + g)
                hi, src, lo = key_parts(g)
                V_.scalar_tensor_tensor(lo, src, wqk[:, 0:1], hi, ALU.mult, ALU.subtract).then_inc(s_lo, 1)
            dve.wait_ge(s_ps, G_CKT + 1)
            hi, src, lo = key_parts(4)
            V_.tensor_scalar(ckTv[:, :, :].rearrange("p b n -> p (b n)"), src, kw[:, 0:1], None, ALU.mult).then_inc(s_setd, 1)
            dve.wait_ge(s_hi, 10)
            V_.scalar_tensor_tensor(lo, src, wqk[:, 0:1], hi, ALU.mult, ALU.subtract).then_inc(s_lo, 1)
            for g in ours(1, G_CW, 8):
                evac(G_CW + g, CW[:, g // 4, 2 * (g % 4):2 * (g % 4) + 2, :], two(G_CW + g))
            if G_FS % 2 == 1:
                evac(G_FS, fscale[:, :], bank(G_FS % 8)[:, 0:1], 1.0 / (HID * HID))
            copied(dve, G_FS)
            link(V_.tensor_scalar(fthr[:, :], fscale[:, :], 1e-10, 0.5, ALU.add, ALU.mult))
            link(V_.tensor_scalar(fthn[:, :], fthr[:, :], -1.0, None, ALU.mult))
            V_.tensor_scalar(fw_a[:, :, :], fw_s[:, :, :], fthr[:, 0:1], fscale[:, 0:1], ALU.is_gt, ALU.mult)
            link(V_.tensor_scalar(fw_b[:, :, :], fw_s[:, :, :], fthn[:, 0:1], fscale[:, 0:1], ALU.is_lt, ALU.mult))
            V_.tensor_tensor(fw_s[:, :, :], fw_a[:, :, :], fw_b[:, :, :], ALU.subtract).then_inc(s_fw, 1)
            if G_FT % 2 == 1:
                evac(G_FT, wfT[:, :, :], two(G_FT))
            copied(dve, G_END - 1)
            copied(dve, G_END - 2)
            dve.wait_ge(s_e, 2)
            V_.memset(ny[:, :], 1.0).then_inc(s_out, 16)
            V_.memset(nu[:, :], 1.0).then_inc(s_setd, 1)
            link(V_.memset(nx[:, :], 1.0))
            base[0], since[0] = base[0] + since[0], 0
            NORM1, NORM2 = HEADS, HEADS + 1

            def step(i, front, mid, proj, ffn, last_norm):
                q = (nx[:, 0:HEADS + 2], ny[:, 0:HEADS + 2], nu[:, 0:HEADS + 2])
                S = bank(5, 2).rearrange("p (a n) -> p a n", n=NBLK)
                norms = front or ffn or last_norm
                if front:
                    t = i + 1
                    for hf in range(2):
                        dve.wait_ge(a_sq, 2 * t + hf + 1)
                        V_.tensor_reduce(ssq[:, 8 * hf:8 * hf + 8], sq[:, 8 * hf:8 * hf + 8, :], AX.X, ALU.add).then_inc(d_red, 1)
                    dve.wait_ge(d_red, 2 * t + 2)
                    chained(V_.tensor_scalar(nx[:, 0:HEADS], ssq[:, :], 1.0 / D, 1e-6, ALU.mult, ALU.add))
                if norms:
                    for n in range(4):
                        rsqrt_part(n, *q)
                if mid:
                    dve.wait_ge(p_cs, i + 1)
                    chained(V_.tensor_reduce(mc[:, :], S, AX.X, ALU.max))
                    after_link()
                    chained(V_.tensor_tensor(mm[:, :], mc[:, :], sinkr[:, :], ALU.max))
                    after_link()
                    wait(dve, a_ec, i)
                    V_.tensor_scalar(mn[:, :], mm[:, :], -SCALE, None, ALU.mult).then_inc(d_cmax, 1)
                    dve.wait_ge(d_cmax, i + 1)
                    wait(dve, a_ecs, i)
                    V_.tensor_tensor(cm[:, :], sinkb[:, :], mn[:, :], ALU.add).then_inc(d_cm, 1)
                if norms:
                    for n in range(4, 11):
                        rsqrt_part(n, *q)
                    after_link()
                if front:
                    wait(dve, p_qt, 2 * t)
                    for hf in range(2):
                        heads = slice(8 * hf, 8 * hf + 8)
                        V_.tensor_tensor(qs[:, heads, :], qbank(hf).rearrange("p (a d) -> p a d", d=D),
                                         ny[:, heads].unsqueeze(2).to_broadcast([P, 8, D]), ALU.mult).then_inc(d_qs, 1)
                    dve.wait_ge(d_qs, 2 * t + 2)
                    wait(dve, g_rope, 2 * t)
                    tab = rope_s[:, ds(t % TPB, 1), :]
                    V_.tensor_tensor(rt1[:, :, :], qs[:, :, 0:ROPE], tab[:, :, 0:64].to_broadcast([P, HEADS, 64]),
                                     ALU.mult).then_inc(d_rope, 1)
                if ffn:
                    wait(dve, p_xt, i - 2)
                    V_.tensor_scalar(x1[:, :], y[:, :], mv[:, 0, 0:1], ny[:, NORM1:NORM1 + 1], ALU.subtract,
                                     ALU.mult).then_inc(d_x1, 1)
                if last_norm:
                    t3 = i - 3
                    dve.wait_ge(s_out, 16 * t3 + 16)
                    V_.tensor_scalar(res[:, :], z[:, :], mv[:, 1, 0:1], ny[:, NORM2:NORM2 + 1], ALU.subtract,
                                     ALU.mult).then_inc(d_out, 1)
                if mid:
                    dve.wait_ge(a_ec, i + 1)
                    dve.wait_ge(a_ecs, i + 1)
                    chained(V_.tensor_tensor(dc[:, :], sc[:, :], es[:, :], ALU.add))
                    after_link()
                    wait(dve, g_cn, i)
                    V_.reciprocal(rc[:, :], dc[:, :]).then_inc(d_rc, 1)

                def divide(c):
                    dve.wait_ge(p_pv, 2 * i + c + 1)
                    parts = []
                    for kb, n in enumerate((3, 3, 2)):
                        parts.append((slice(3 * kb, 3 * kb + n), n,
                                      bank((4, 0)[c] + kb)[:, 0:n * VW].rearrange("p (a d) -> p a d", d=VW)))
                    for pairs, n, pv in parts:
                        last = V_.tensor_tensor(dn[:, pairs], pv[:, :, D], e0[:, pairs], ALU.mult)
                    link(last)
                    link(V_.tensor_tensor(dn2[:, :], dn[:, :], e1[:, :], ALU.add))
                    link(V_.reciprocal(dn3[:, :], dn2[:, :]))
                    link(V_.tensor_tensor(r8[:, :], dn3[:, :], e0[:, :], ALU.mult))
                    wait(dve, p_at, 2 * i + c - 1)
                    for pairs, n, pv in parts:
                        last = V_.tensor_tensor(ao[:, c, pairs, :], pv[:, :, 0:D],
                                                r8[:, pairs].unsqueeze(2).to_broadcast([P, n, D]), ALU.mult)
                    last.then_inc(d_ao, 1)
                    dve.wait_ge(d_ao, 2 * i + c + 1)

                if mid:
                    divide(0)
                if front:
                    for hf in range(2):
                        heads = slice(8 * hf, 8 * hf + 8)
                        dve.wait_ge(a_qt, 2 * i + 3 + hf)
                        V_.tensor_tensor(qT[:, 1, heads, :], qbank(hf).rearrange("p (a q) -> p a q", q=P),
                                         qT[:, 0, heads, :], ALU.subtract).then_inc(d_ql, 1)
                if proj:
                    dve.wait_ge(p_o, i)
                    if ffn:
                        dve.wait_ge(d_x1, i - 1)
                    V_.tensor_tensor(y[:, :], bank(7)[:, 0:HID], H[:, ds(i - 1, 1), :].rearrange("p a n -> p (a n)"),
                                     ALU.add).then_inc(d_y, 1)
                if mid:
                    divide(1)
                if ffn:
                    dve.wait_ge(p_f, i - 1)
                    dve.wait_ge(d_x1, i - 1)
                    if last_norm:
                        dve.wait_ge(d_out, i - 2)
                    V_.tensor_tensor(z[:, :], bank(7)[:, HID:2 * HID], x1[:, :], ALU.add).then_inc(d_fr, 1)
                if ffn:
                    dve.wait_ge(d_fr, i - 1)
                    chained(V_.tensor_tensor(z[:, :], z[:, :], fb_s[:, :], ALU.add))
                if proj:
                    dve.wait_ge(d_y, i)
                    chained(V_.bn_stats(bns[:, 0, :], y[:, :]))
                if ffn:
                    after_link()
                    chained(V_.bn_stats(bns[:, 1, :], z[:, :]))
                if proj or ffn:
                    after_link()
                    V_.memset(nu[:, 0:1], 0.0)
                    sets = slice(0 if proj else 1, 2 if ffn else 1)
                    for n in range(sets.start, sets.stop):
                        chained(V_.bn_aggr(mv[:, n, :], bns[:, n, :]))
                    after_link()
                    chained(V_.tensor_scalar(nx[:, HEADS + sets.start:HEADS + sets.stop], mv[:, sets, 1], 1e-5, None, ALU.add))
                    after_link()

            LINKS = 1 + 11 + 2 + 1 + 4 + 3 + 2 + 1 + 4

            def counted(i, *stages):
                if isinstance(i, int):
                    step(i, *stages)
                    base[0], since[0] = base[0] + since[0], 0
                    return
                before = base[0]
                base[0] = before + (i - 3) * LINKS
                step(i, *stages)
                assert since[0] == LINKS, since[0]
                base[0], since[0] = before + (NT - 4) * LINKS, 0

            all_steps(counted, dve)

        @block_ctx.gpsimd
        def _(pool):
            G = nc.gpsimd
            G.memset(ident[:, :], 0.0).then_inc(s_setp, 1)
            for k in range(KC):
                for bt in range(BATCH):
                    last = G.memset(hT[:, k, bt, 0:WIN], 0.0)
            last.then_inc(s_idb, 1)
            for bt in range(BATCH):
                last = G.memset(kT[:, :, bt * SPAN:bt * SPAN + WIN], 0.0)
            last.then_inc(s_setp, 1)
            pool.wait_ge(s_setp, 2)
            G.affine_select(out=ident[:, :], in_=ident[:, :], compare_op=ALU.not_equal, fill=1.0,
                            base=0, pattern=[[-1, P]], channel_multiplier=1).then_inc(s_id, 1)
            pool.wait_ge(s_id, 2)
            G.tensor_copy(identb[:, :], ident[:, :]).then_inc(s_setp, 1)
            pool.wait_ge(s_tab, 48)

            def step(i, front, mid, proj, ffn, last_norm):
                def mask(c):
                    pool.wait_ge(a_es, 2 * i + c + 1)
                    wait(pool, p_pv, 2 * i + c - 1)
                    keep = window_s[:, 1:2, :] if c else window_s[:, ds(i % TPB, 1), :]
                    G.tensor_tensor(Pm[:, c, :, :], E[:, c, :, :], keep.to_broadcast([P, HEADS, WIN]),
                                    ALU.mult).then_inc(g_mask, 1)

                if mid:
                    mask(0)
                if front:
                    for hf in range(2):
                        heads = slice(8 * hf, 8 * hf + 8)
                        pool.wait_ge(d_qs, 2 * i + 3 + hf)
                        if hf == 0:
                            tab = rope_s[:, ds((i + 1) % TPB, 1), :]
                        else:
                            G.tensor_tensor(spare[:, :], ones[:, 0:1], ones[:, 0:1], ALU.mult)
                        G.tensor_tensor(rt2[:, heads, 0:32], qs[:, heads, 32:64], tab[:, :, 64:96].to_broadcast([P, 8, 32]),
                                        ALU.mult)
                        G.tensor_tensor(rt2[:, heads, 32:64], qs[:, heads, 0:32], tab[:, :, 96:128].to_broadcast([P, 8, 32]),
                                        ALU.mult).then_inc(g_rt, 1)
                    pool.wait_ge(d_rope, i + 2)
                    for hf in range(2):
                        heads = slice(8 * hf, 8 * hf + 8)
                        pool.wait_ge(g_rt, 2 * i + 3 + hf)
                        G.tensor_tensor(qs[:, heads, 0:ROPE], rt1[:, heads, :], rt2[:, heads, :], ALU.add).then_inc(g_rope, 1)
                if mid:
                    mask(1)
                    pool.wait_ge(d_rc, i + 1)
                    wait(pool, p_ct, 2 * i)
                    G.tensor_tensor(Pn[:, :, :], Ec[:, :, :], rc[:, :].unsqueeze(2).to_broadcast([P, HEADS, NBLK]),
                                    ALU.mult).then_inc(g_cn, 1)

            all_steps(step, pool)


_INS = ["L0_attn_h", "L0_attn_Wq_c", "L0_attn_Wq_up", "L0_attn_Wk", "L0_attn_Wv", "L0_attn_W_comp",
        "L0_attn_q_norm_w", "L0_attn_k_norm_w", "L0_attn_sink", "L0_attn_Wg", "L0_attn_Wo",
        "L0_ffn_weight", "L0_ffn_bias"]


def kernel(**inputs):
    import numpy as _np
    import concourse.bacc as _bacc
    from concourse import mybir as _mybir
    from concourse.bass_utils import run_bass_kernel_spmd as _run

    nc = _bacc.Bacc("TRN2", target_bir_lowering=False, num_devices=1)
    arrays = {f"in_{n}": _np.ascontiguousarray(inputs[n]) for n in _INS}
    for name, table in zip(("rope", "block", "window"), shape_tables()):
        arrays[f"table_{name}"] = table
    args = [nc.dram_tensor(n, a.shape, _mybir.dt.from_np(a.dtype), kind="ExternalInput").ap()
            for n, a in arrays.items()]
    out = nc.dram_tensor("out", (BATCH, SEQ, HID), _mybir.dt.float32, kind="ExternalOutput").ap()
    build(nc, *args, out)
    return _run(nc, [arrays], core_ids=[0]).results[0]["out"]
```

```python
from contextlib import ExitStack

import concourse.bass as bass
import numpy as np
from concourse import mybir

BATCH, SEQ, HID = 2, 1024, 256
HEADS, D, QC = 16, 128, 64
BLK, WIN = 16, 64
ROPE = 64
GROUPS, INTER = 4, 256
CAP = 50.0
P = 128
NT = BATCH * SEQ // P
EARLY = 2
TPB = SEQ // P
NBLK = SEQ // BLK
PAIRS = HEADS // 2
KC = HID // P
VW = D + 1
SPAN = WIN + SEQ
SCALE = float(D) ** -0.5
TAB = 2 * ROPE
MASKED = -1e30


def shape_tables():
    inv = np.float32(1.0) / np.float32(10000.0) ** (np.arange(0, ROPE, 2, dtype=np.float32) / np.float32(ROPE))
    ang = np.arange(SEQ, dtype=np.float32)[:, None] * inv[None, :].astype(np.float32)
    cos, sin = np.cos(ang), np.sin(ang)
    rope = np.concatenate([cos, cos, -sin, sin], 1).astype(np.float32)
    rope = rope.reshape(TPB, P, TAB).transpose(1, 0, 2).copy()
    t = np.arange(SEQ)
    end = np.arange(NBLK) * BLK + BLK - 1
    block = np.where(end[None] < t[:, None], 0.0, MASKED).astype(np.float32)
    block = block.reshape(TPB, P, NBLK).transpose(1, 0, 2).copy()
    p, q = np.arange(P)[:, None], np.arange(WIN)[None]
    usual = ((p > q) & (p <= q + WIN)).astype(np.float32)
    first = usual * (p >= WIN)
    window = np.stack([first] + [usual] * (TPB - 1), 1).astype(np.float32)
    return rope, block, np.ascontiguousarray(window)


def build(nc, h, wqc, wqup, wk, wv, wcomp, qnw, knw, sink, wg, wo, fw, fb, rope_t, block_t, window_t, out):
    f32, bf16, i32 = mybir.dt.float32, mybir.dt.bfloat16, mybir.dt.int32
    f32r, f16 = mybir.dt.float32r, mybir.dt.float16
    ALU, ACT, AX = mybir.AluOpType, mybir.ActivationFunctionType, mybir.AxisListType
    ds = bass.ds

    h_v = h.rearrange("b (j p) c -> p (b j) c", p=P)
    out_v = out.rearrange("b s c -> (b s) c")

    ctx = ExitStack()
    with ctx:
        def sb(name, shape, dt=f32):
            return ctx.enter_context(nc.sbuf_tensor(name, shape, dt))

        def sem(name):
            return ctx.enter_context(nc.semaphore(name))

        H = sb("H", [P, NT, HID])
        ident, identb = sb("ident", [P, P]), sb("identb", [P, P], bf16)
        rope_s = sb("rope_s", [P, TPB, TAB])
        block_b = sb("block_b", [P, TPB, NBLK], bf16)
        window_s = sb("window_s", [P, TPB, WIN])
        wqup_p = sb("wqup_p", [P, 2, HEADS * D], f32r)
        xcT = sb("xcT", [P, (NT + 1) * P], f32r)
        kT = sb("kT", [P, 2, BATCH * SPAN], f16)
        V = sb("V", [P, 2 * NT, VW])
        ckTs = sb("ckTs", [P, 2, BATCH * NBLK], f16)
        ckTv = sb("ckTv", [P, 2, BATCH * NBLK], f32r)
        Weff = sb("Weff", [P, 2, HEADS, HID], f32r)
        CW = sb("CW", [P, BATCH, PAIRS, HID])
        wfT = sb("wfT", [P, KC, HID])
        fb_s = sb("fb_s", [P, HID])
        sinkb, sinkr = sb("sinkb", [P, HEADS]), sb("sinkr", [P, HEADS])
        e0, e1, skp, skm = (sb(n, [P, PAIRS]) for n in ("e0", "e1", "skp", "skm"))
        qw, kw, wqk = (sb(n, [P, 1]) for n in ("qw", "kw", "wqk"))

        room_h, room_comp, room_wg = (sb(n, [P, w]) for n, w in (
            ("room_h", KC * BATCH * SEQ), ("room_comp", BLK * KC * D), ("room_wg", HEADS * INTER)))
        with nc.sbuf_tensor("room_wgT", [P, KC * HEADS * P], f32) as room_wgT:
            pass
        aoT = sb("aoT", [P, 2, PAIRS, 2, 2, WIN], f32r)
        hT = room_h[:, :].rearrange("p (k b s) -> p k b s", k=KC, b=BATCH)
        wcomp_s = room_comp[:, :].rearrange("p (m d) -> p m d", d=D)
        wg_s = room_wg[:, :].rearrange("p (f i) -> p f i", i=INTER)
        wgT = room_wgT[:, :].rearrange("p (k f) -> p k f", k=KC)
        room_wo, room_K = sb("room_wo", [P, GROUPS * KC * HID]), sb("room_K", [P, (NT + 1) * D])
        wo_s = room_wo[:, :].rearrange("p (k n) -> p k n", n=HID)
        K = room_K[:, :].rearrange("p (t d) -> p t d", d=D)
        fsum, fscale, fthr, fthn = (sb(n, [P, 1]) for n in ("fsum", "fscale", "fthr", "fthn"))

        def part(room, start, pattern, size=HEADS * D, **axes):
            return room[:, start:start + size].rearrange(pattern, **axes)

        sq = part(room_wg, 0, "p (a d) -> p a d", d=D)
        sqk = part(room_wgT, 0, "p (a d) -> p a d", d=D)
        rt1 = part(room_comp, 2048, "p (a d) -> p a d", HEADS * ROPE, d=ROPE)
        rt2 = part(room_comp, 3072, "p (a d) -> p a d", HEADS * ROPE, d=ROPE)
        wqup_s, rest = (CW[:, n, :, :].rearrange("p a n -> p (a n)") for n in range(2))
        fw_s = part(rest, 0, "p (k n) -> p k n", KC * HID, k=KC)
        wk_s, wv_s = (part(rest, 512 + 256 * n, "p (k n) -> p k n", KC * D, k=KC) for n in range(2))
        wqc_s = part(rest, 1024, "p (k n) -> p k n", KC * QC, k=KC)
        ckr, ones = rest[:, 1152:1280], rest[:, 1280:1408]
        block_f = part(rest, 1408, "p (t n) -> p t n", TPB * NBLK, t=TPB)
        fw_a, fw_b = (part(room_comp, 512 * n, "p (k n) -> p k n", KC * HID, k=KC) for n in range(2))
        E = part(room_comp, 0, "p (c a q) -> p c a q", c=2, q=WIN)
        Pm = part(room_wg, 0, "p (c a q) -> p c a q", c=2, q=WIN)
        ao = part(room_wg, 2048, "p (c a d) -> p c a d", c=2, d=D)
        qs = part(room_K, 0, "p (a d) -> p a d", d=D)
        qT = part(room_h, 0, "p (h a q) -> p h a q", h=2, q=P // 2).bitcast(f16)
        Ec = part(room_h, 3072, "p (a n) -> p a n", HEADS * NBLK, n=NBLK)
        xcF = sb("xcF", [P, P], f32r)
        x1T = part(room_h, 2048, "p (k n) -> p k n", KC * P, k=KC)
        kTw = part(room_h, 2304, "p (h n) -> p h n", P + WIN, h=2).bitcast(f16)
        x1b = room_h[:, 2624:2880]
        y, z, x1, res = (room_wo[:, HID * n:HID * (n + 1)] for n in range(4))
        PcT = part(room_wo, 1024, "p (a q) -> p a q", PAIRS * P, q=P)
        ssk = sb("ssk", [P, NT + 1])
        ssq = sb("ssq", [P, HEADS])
        mc, mm, mn, cm, es, sc, dc, rc = (room_h[:, 2880 + HEADS * n:2880 + HEADS * (n + 1)] for n in range(8))
        spare = sb("spare", [P, 1])
        dn, dn2, dn3, r8 = (sb(n, [P, PAIRS]) for n in ("dn", "dn2", "dn3", "r8"))
        bns, mv = sb("bns", [P, 2, 6]), sb("mv", [P, 2, 2])
        nx, ny, nu, nt = (sb(n, [P, NT + 2]) for n in ("nx", "ny", "nu", "nt"))

        PS = ctx.enter_context(nc.psum_tensor("PS", [P, 8 * 512], f32))

        def bank(b, n=1):
            return PS[:, 512 * b:512 * (b + n)]

        s_h = [sem(f"s_h{g}") for g in range(4)]
        s_tab, s_blk, s_comp, s_wg, s_wo, s_wk, s_wqc, s_wv, s_wq, s_small = (sem(n) for n in (
            "s_tab", "s_blk", "s_comp", "s_wg", "s_wo", "s_wk", "s_wqc", "s_wv", "s_wq", "s_small"))
        s_id = sem("s_id")
        s_ps = sem("s_ps")
        s_eva, s_evd = sem("s_eva"), sem("s_evd")
        s_hi, s_lo = sem("s_hi"), sem("s_lo")
        s_wh, s_wl = sem("s_wh"), sem("s_wl")
        s_sq, s_ks, s_kr, s_kn = (sem(n) for n in (
            "s_sq", "s_ks", "s_kr", "s_kn"))
        s_fs, s_fw = sem("s_fs"), sem("s_fw")
        s_sm, s_e = sem("s_sm"), sem("s_e")
        s_setp, s_sets, s_setd = sem("s_setp"), sem("s_sets"), sem("s_setd")
        p_q, p_sw, p_cs, p_o, p_qt, p_pv, p_ct, p_at, p_xt, p_f = (sem(n) for n in (
            "p_q", "p_sw", "p_cs", "p_o", "p_qt", "p_pv", "p_ct", "p_at", "p_xt", "p_f"))
        a_sq, a_tanh, a_es, a_ec, a_ecs, a_qt, a_ct, a_at, a_xt, a_xc, a_kw = (sem(n) for n in (
            "a_sq", "a_tanh", "a_es", "a_ec", "a_ecs", "a_qt", "a_ct", "a_at", "a_xt", "a_xc", "a_kw"))
        d_red, d_qs, d_rope, d_add, d_cmax, d_cm, d_rc, d_ql, d_ao, d_al, d_x1, d_fr, d_y, d_out = (sem(n) for n in (
            "d_red", "d_qs", "d_rope", "d_add", "d_cmax", "d_cm", "d_rc", "d_ql", "d_ao", "d_al", "d_x1", "d_fr",
            "d_y", "d_out"))
        g_mask, g_cn, g_rt, g_xb = (sem(n) for n in ("g_mask", "g_cn", "g_rt", "g_xb"))
        s_out = sem("s_out")
        s_chain = sem("s_chain")

        def qbank(hf):
            return bank(2 - 2 * hf, 2)

        def ffn_bank(mid):
            return bank(7) if mid else bank(6)

        def wait(eng, s, value):
            if not isinstance(value, int) or value > 0:
                eng.wait_ge(s, value)

        NAMES = ("H", 8), ("K", 4), ("CR", 1), ("CK", 1), ("XC", 4), ("V", 4), ("FS", 1), ("KT", 4), ("CKT", 1), \
            ("WG", 8), ("WE", 8), ("CW", 8), ("FT", 1)
        starts = dict(zip((n for n, _ in NAMES), np.cumsum([0] + [c for _, c in NAMES]).tolist()))
        G_H, G_K, G_CR, G_CK, G_XC, G_V, G_FS, G_KT, G_CKT, G_WG, G_WE, G_CW, G_FT = starts.values()
        by_scalar = [g % 2 == 0 if g < G_CW else g - G_CW not in (2, 4, 6) for g in range(G_FT + 1)]

        def gbank(g):
            return bank(7 if g == G_FT else 4 + (g - G_WE) % 4 if g >= G_WE else g % 8)

        def ours(mine, start, n):
            return [g for g in range(n) if by_scalar[start + g] != bool(mine)]

        def two(g):
            return gbank(g).rearrange("p (k n) -> p k n", k=2)

        def four(g):
            return gbank(g).rearrange("p (t d) -> p t d", d=D)

        def key_parts(g):
            if g == 4:
                return ckTs[:, 0, :], gbank(G_CKT)[:, 0:P], ckTs[:, 1, :]
            at = (g // 2) * SPAN + WIN + (g % 2) * 512
            return kT[:, 0, at:at + 512], gbank(G_KT + g), kT[:, 1, at:at + 512]

        def values(eng, copy, signal, g):
            eng.wait_ge(s_ps, G_V + g + 1)
            t, v = 4 * g, four(G_V + g)
            w = V[:, :, 0:D].rearrange("p (t c) d -> p c t d", c=2)
            n = 3 if g % 2 else 4
            copy(w[:, 1, t:t + 4, :], v)
            copy(w[64:P, 0, t:t + 4, :], v[0:64, :, :])
            copy(w[0:64, 0, t + 1:t + 1 + n, :], v[64:P, 0:n, :]).then_inc(signal, 1)

        def value_weights(eng, copy, signal, mine):
            for g in ours(mine, G_CW, 8):
                eng.wait_ge(s_ps, G_CW + g + 1)
                for b in range(BATCH):
                    for par in range(2):
                        last = copy(CW[par * 64:par * 64 + 64, b, g, :], two(G_CW + g)[b * NBLK:(b + 1) * NBLK, par, :])
                last.then_inc(signal, 1)

        def copied(eng, g):
            if g < 0:
                return
            for first, n, at in ((G_XC, 4, 1), (G_KT, 5, 5)):
                if first <= g < first + n:
                    eng.wait_ge(s_lo, at + g - first + 1)
                    return
            if G_WE <= g < G_CW:
                eng.wait_ge(s_wl, g - G_WE + 1)
                return
            before = [x for x in range(g + 1) if not (G_WE <= x < G_CW or G_XC <= x < G_XC + 4 or G_KT <= x < G_KT + 5)]
            eng.wait_ge(s_eva if by_scalar[g] else s_evd, sum(by_scalar[x] == by_scalar[g] for x in before))

        PARTS = ((0, 0), (1, 0), (0, 1))

        def all_steps(body, eng):
            def at(i):
                body(i, *(0 <= i + 1 - n < NT for n in range(5)))

            for i in range(-1, 3):
                at(i)
            with eng.Fori(3, NT - 1) as i:
                body(i, *[True] * 5)
            for i in range(NT - 1, NT + 3):
                at(i)

        block_ctx = ctx.enter_context(nc.Block())

        @block_ctx.sync
        def _(sp):
            for g in range(4):
                sp.dma_start(H[:, 4 * g:4 * g + 4, :], h_v[:, 4 * g:4 * g + 4, :]).then_inc(s_h[g], 16)
            sp.dma_start(wcomp_s[:, :, :], wcomp.rearrange("(m p) d -> p m d", p=P)).then_inc(s_comp, 16)
            sp.dma_start(rope_s[:, :, :], rope_t).then_inc(s_tab, 16)
            sp.dma_start(wg_s[:, :, :], wg.rearrange("g (f p) i -> p (g f) i", p=P)).then_inc(s_wg, 16)
            sp.dma_start(wo_s[:, :, :], wo.rearrange("(k p) n -> p k n", p=P)).then_inc(s_wo, 16)
            sp.dma_start(window_s[:, :, :], window_t).then_inc(s_tab, 16)
            sp.wait_ge(d_out, 1)
            sp.dma_start(out_v[0:P, :], res[:, :]).then_inc(s_out, 16)
            with sp.Fori(1, NT) as i:
                row = sp.snap(i * P)
                sp.wait_ge(d_out, i + 1)
                sp.dma_start(out_v[ds(row, P), :], res[:, :]).then_inc(s_out, 16)
            sp.wait_ge(s_out, 16 * NT + 16)

        @block_ctx.tensor
        def _(pe):
            made = [0]

            def begin(g):
                assert g == made[0]
                if g < G_WE:
                    copied(pe, g - 8)
                return gbank(g)

            def end(ins):
                ins.then_inc(s_ps, 1)
                made[0] += 1

            pe.wait_ge(s_id, 2)
            for g in range(8):
                pe.wait_ge(s_h[g // 2], 16)
                b = begin(G_H + g)
                for k in range(KC):
                    for t in range(2):
                        last = nc.tensor.transpose(b[:, (2 * k + t) * P:(2 * k + t + 1) * P],
                                                   H[:, 2 * g + t, k * P:(k + 1) * P], ident[:, :])
                end(last)

            def by_token(start, w):
                for g in range(4):
                    if start == G_K:
                        copied(pe, G_H + 2 * g + 1)
                        copied(pe, G_H + 2 * g)
                    b = begin(start + g)
                    for t in range(4 * g, 4 * g + 4):
                        at = (t % TPB) * P
                        for k in range(KC):
                            last = nc.tensor.matmul(b[:, (t % 4) * D:(t % 4 + 1) * D], hT[:, k, t // TPB, at:at + P],
                                                    w[:, k, :], start=k == 0, stop=k == KC - 1)
                    end(last)

            pe.wait_ge(s_wk, 16)
            by_token(G_K, wk_s)
            b = begin(G_CR)
            pe.wait_ge(s_comp, 16)
            for m in range(BLK):
                for k in range(KC):
                    rows = hT[:, k, :, :].rearrange("p b (n m) -> p b n m", m=BLK)[:, :, :, m]
                    last = nc.tensor.matmul(b[:, 0:P], wcomp_s[:, KC * m + k, :], rows,
                                            start=m == k == 0, stop=m == BLK - 1 and k == KC - 1)
            end(last)
            copied(pe, G_CR)
            b = begin(G_CK)
            end(nc.tensor.transpose(b[:, 0:D], ckr[:, :], ident[:, :]))
            pe.wait_ge(s_wqc, 16)
            for g in range(4):
                b = begin(G_XC + g)
                at = (g % 2) * 512
                for k in range(KC):
                    last = nc.tensor.matmul(b[0:QC, :], wqc_s[:, k, :], hT[:, k, g // 2, at:at + 512],
                                            start=k == 0, stop=k == KC - 1)
                end(last)
            pe.wait_ge(s_wv, 16)
            by_token(G_V, wv_s)
            pe.wait_ge(s_fs, 1)
            b = begin(G_FS)
            end(nc.tensor.matmul(b[:, 0:1], ones[:, :], fsum[:, :], start=True, stop=True))
            pe.wait_ge(s_kn, 1)
            for g in range(4):
                b = begin(G_KT + g)
                for t in range(4):
                    last = nc.tensor.transpose(b[:, t * P:(t + 1) * P], K[:, 4 * g + t, :], ident[:, :])
                end(last)
            b = begin(G_CKT)
            end(nc.tensor.transpose(b[:, 0:P], K[:, NT, :], ident[:, :]))
            pe.wait_ge(s_wg, 16)
            for g in range(8):
                b = begin(G_WG + g)
                for k in range(KC):
                    for f in range(2):
                        last = nc.tensor.transpose(b[:, (2 * k + f) * P:(2 * k + f + 1) * P],
                                                   wg_s[:, 2 * g + f, k * P:(k + 1) * P], ident[:, :])
                end(last)
            for g in range(G_WE - 8, G_WE):
                copied(pe, g)

            def output_weights():
                pe.wait_ge(s_wo, 16)
                for g in range(8):
                    copied(pe, G_WG + g)
                    if g >= 4:
                        copied(pe, G_WE + g - 4)
                    b = begin(G_WE + g)
                    for f in range(2):
                        hd = 2 * g + f
                        for k in range(KC):
                            last = nc.tensor.matmul(b[:, f * HID:(f + 1) * HID], wgT[:, k, hd * P:(hd + 1) * P],
                                                    wo_s[:, (hd // GROUPS) * KC + k, :], start=k == 0, stop=k == KC - 1)
                    end(last)

            def ffn_weights():
                pe.wait_ge(s_fw, 1)
                b = begin(G_FT)
                for k in range(KC):
                    for o in range(KC):
                        last = nc.tensor.transpose(b[:, (2 * k + o) * P:(2 * k + o + 1) * P],
                                                   wfT[:, o, k * P:(k + 1) * P], ident[:, :])
                end(last)

            def value_weights():
                pe.wait_ge(s_setd, 1)
                for g in range(8):
                    copied(pe, G_WE + g)
                    copied(pe, G_CW + g - 4)
                    b = begin(G_CW + g)
                    for f in range(2):
                        for n, (kp, wp) in enumerate(PARTS):
                            last = nc.tensor.matmul(b[:, f * HID:(f + 1) * HID], ckTv[:, kp, :], Weff[:, wp, 2 * g + f, :],
                                                    start=n == 0, stop=n == 2)
                    end(last)

            def step(i, front, mid, proj, ffn, last_norm):
                if front:
                    pe.wait_ge(a_xc, i + 2)
                    if isinstance(i, int):
                        wait(pe, d_ql, 2 * i + 2)
                    for hf in range(2):
                        wait(pe, *((a_ct, 2 * i) if hf else (d_al, 2 * i - 1)))
                        for n in (2 * hf, 2 * hf + 1):
                            for w in range(2):
                                last = nc.tensor.matmul(qbank(hf)[:, (n % 2) * 512:(n % 2 + 1) * 512], xcF[:, :], wqup_p[:, w, n * 512:(n + 1) * 512],
                                                        start=w == 0, stop=w == 1)
                        last.then_inc(p_q, 1)
                if isinstance(i, int) and i == 0:
                    copied(pe, G_CW + 6)
                    copied(pe, G_CW + 7)
                    pe.wait_ge(s_sets, 1)
                    pe.wait_ge(s_setd, 2)
                if mid:
                    pe.wait_ge(a_kw, i + 1)
                    pe.wait_ge(d_ql, 2 * i + 2)
                    for u, b in enumerate((6, 4, 5, 6)):
                        wait(pe, *((d_ao, 2 * i), (d_al, 2 * i), (d_al, 2 * i), (a_tanh, 4 * i + 1))[u])
                        c, hf = divmod(u, 2)
                        for n, (kp, qp) in enumerate(PARTS):
                            last = nc.tensor.matmul(bank(b), kTw[:, kp, c * WIN:c * WIN + P],
                                                    qT[:, qp, 8 * hf:8 * hf + 8, c * WIN:(c + 1) * WIN],
                                                    start=n == 0, stop=n == 2)
                        last.then_inc(p_sw, 1)
                    blocks = (i // TPB) * NBLK
                    maskrow = block_b[:, ds(i % TPB, 1), :].to_broadcast([P, 8, NBLK])
                    for hf in range(2):
                        pe.wait_ge(a_tanh, 4 * i + 2 + hf)
                        nc.tensor.matmul(bank(4 + hf), identb[:, :], maskrow, start=True, stop=True)
                        for hd in range(8):
                            for kp, qp in PARTS:
                                last = nc.tensor.matmul(bank(4 + hf)[:, hd * NBLK:(hd + 1) * NBLK],
                                                        qT[:, qp, 8 * hf + hd, :], ckTs[:, kp, ds(blocks, NBLK)],
                                                        start=False, stop=True, skip_group_check=True)
                    last.then_inc(p_cs, 1)
                if isinstance(i, int) and i == 0:
                    ffn_weights()
                if isinstance(i, int) and i == -1:
                    output_weights()
                o = bank(7)[:, 0:HID]

                def ffn_input():
                    pe.wait_ge(d_x1, i - 1)
                    wait(pe, d_fr, i - 2)
                    if mid:
                        wait(pe, d_y, i if proj else NT)
                    for k in range(KC):
                        last = nc.tensor.transpose(ffn_bank(mid)[:, HID + k * P:HID + (k + 1) * P],
                                                   x1[:, k * P:(k + 1) * P], ident[:, :])
                    last.then_inc(p_xt, 1)

                def ffn_matmul():
                    pe.wait_ge(a_xt, i - 1)
                    for k in range(KC):
                        last = nc.tensor.matmul(ffn_bank(mid)[:, HID:2 * HID], x1T[:, k, :], wfT[:, k, :],
                                                start=k == 0, stop=k == KC - 1)
                    last.then_inc(p_f, 1)

                def project_blocks(start, pairs=range(PAIRS)):
                    if pairs[0] == 0:
                        pe.wait_ge(a_ct, 2 * t + 2)
                    bt = t // TPB
                    for pr in pairs:
                        last = nc.tensor.matmul(o, PcT[:, pr, :], CW[:, ds(bt, 1), pr, :],
                                                start=start and pr == 0, stop=not start and pr == PAIRS - 1)
                    return last

                if proj:
                    t = i - 1
                    if isinstance(i, int) and i == 1:
                        copied(pe, G_FT)
                    wait(pe, d_y, t)
                    wait(pe, d_fr, t - 1)
                    if not mid:
                        project_blocks(True)
                    pe.wait_ge(a_at, 2 * t + 2)
                    pe.wait_ge(d_al, 2 * t + 2)
                    for hd in range(HEADS):
                        if not mid and hd == HEADS // 2:
                            ffn_input()
                        if not mid and hd == 3 * HEADS // 4:
                            ffn_matmul()
                        for n, (ap, wp) in enumerate(PARTS):
                            last = nc.tensor.matmul(o, aoT[:, ap, hd // 2, hd % 2, :, :].rearrange("p c q -> p (c q)"),
                                                    Weff[:, wp, hd, :], start=mid and hd == n == 0,
                                                    stop=not mid and hd == HEADS - 1 and n == 2)
                    if not mid:
                        last.then_inc(p_o, 1)

                def values(c):
                    pe.wait_ge(g_mask, 2 * i + c + 1)
                    if c == 0:
                        pe.wait_ge(a_tanh, 4 * i + 4)
                    else:
                        pe.wait_ge(d_ao, 2 * i + 1)
                    for pr in (3, 4, 5, 0, 1, 2, 6, 7):
                        if c == 0 and pr == 6 and proj:
                            project_blocks(False, range(EARLY))
                        if c == 0 and pr in (0, 6):
                            pe.wait_ge(a_ec, 2 * i + 1 + pr // 6)
                        pv = bank((4, 6, 5)[pr // 3])[:, (pr % 3) * VW:(pr % 3 + 1) * VW]
                        last = nc.tensor.matmul(pv, Pm[:, c, 2 * pr:2 * pr + 2, :], V[:, ds(2 * i + c, 1), 0:VW],
                                                start=True, stop=True)
                    last.then_inc(p_pv, 1)

                if mid:
                    values(0)
                if front:
                    for hf in range(2):
                        pe.wait_ge(d_add, 2 * i + 3 + hf)
                        pe.wait_ge(d_qs, 2 * i + 3 + hf)
                        for hd in range(8):
                            last = nc.tensor.transpose(qbank(hf)[:, hd * P:(hd + 1) * P],
                                                       qs[:, 8 * hf + hd, :], ident[:, :])
                        last.then_inc(p_qt, 1)
                if isinstance(i, int) and i == -1:
                    value_weights()
                if proj and mid:
                    project_blocks(False, range(EARLY, PAIRS)).then_inc(p_o, 1)
                if mid:
                    values(1)
                if ffn and (mid or not proj):
                    ffn_input()

                def probs_T(n):
                    for pr in range(4 * n, 4 * n + 4):
                        last = nc.tensor.transpose(bank(n)[:, (pr % 4) * P:(pr % 4 + 1) * P],
                                                   Ec[:, 2 * pr:2 * pr + 2, :], ident[:, :])
                    last.then_inc(p_ct, 1)

                def output_T(c):
                    pe.wait_ge(d_ao, 2 * i + c + 1)
                    for pr in range(PAIRS):
                        last = nc.tensor.transpose(bank((2, 4)[c], 2)[:, pr * P:(pr + 1) * P], ao[:, c, pr, :], ident[:, :])
                    last.then_inc(p_at, 1)

                if mid:
                    if front:
                        pe.wait_ge(d_ql, 2 * i + 4)
                    output_T(0)
                    pe.wait_ge(g_cn, i + 1)
                    probs_T(0)
                if ffn and (mid or not proj):
                    ffn_matmul()
                if mid:
                    probs_T(1)
                    output_T(1)

            all_steps(step, pe)

        @block_ctx.scalar
        def _(act):
            act.dma_start(wk_s[:, :, :], wk.rearrange("(k p) n -> p k n", p=P)).then_inc(s_wk, 16)
            act.dma_start(wqc_s[:, :, :], wqc.rearrange("(k p) n -> p k n", p=P)).then_inc(s_wqc, 16)
            for r in range(2):
                act.dma_start(wqup_s[r * QC:(r + 1) * QC, :], wqup).then_inc(s_wq, 16)
            act.dma_start(fw_s[:, :, :], fw.rearrange("(k p) n -> p k n", p=P)).then_inc(s_small, 16)
            act.dma_start(wv_s[:, :, :], wv.rearrange("(k p) n -> p k n", p=P)).then_inc(s_wv, 16)
            act.dma_start(qw[:, :], qnw.rearrange("(p a) -> p a", a=1)).then_inc(s_small, 16)
            act.dma_start(kw[:, :], knw.rearrange("(p a) -> p a", a=1)).then_inc(s_small, 16)
            act.dma_start(sinkb[:, :], sink.partition_broadcast(P)).then_inc(s_small, 16)
            act.dma_start(fb_s[:, :], fb.partition_broadcast(P)).then_inc(s_small, 16)
            act.dma_start(block_f[:, :, :], block_t).then_inc(s_blk, 16)

            def narrow(dst, src, s):
                nc.scalar.activation(dst, src, ACT.Copy).then_inc(s, 1)

            def evac(g, dst, src, scale=1.0):
                act.wait_ge(s_ps, g + 1)
                nc.scalar.mul(dst, src, scale).then_inc(s_eva, 1)

            for g in ours(0, G_H, 8):
                at = (g % 4) * 256
                evac(g, hT[:, :, g // 4, at:at + 256], two(g))
            for g in ours(0, G_K, 4):
                evac(G_K + g, K[:, 4 * g:4 * g + 4, :], four(G_K + g))
            act.wait_ge(s_wq, 32)
            nc.scalar.activation(wqup_p[:, 0, :], wqup_s[:, :], ACT.Copy).then_inc(s_hi, 1)
            copied(act, G_K + 2)
            copied(act, G_K + 3)
            nc.scalar.activation(sqk, K[:, 0:NT, :], ACT.Square).then_inc(s_sq, 1)
            if by_scalar[G_CR]:
                evac(G_CR, ckr[:, :], gbank(G_CR)[:, 0:P])
            if by_scalar[G_CK]:
                evac(G_CK, K[:, NT, :], gbank(G_CK)[:, 0:D])
            for g in range(4):
                act.wait_ge(s_ps, G_XC + g + 1)
                nc.scalar.activation(xcT[0:QC, g * 512:(g + 1) * 512], gbank(G_XC + g)[0:QC, :],
                                     ACT.Copy).then_inc(s_hi, 1)
            act.wait_ge(s_blk, 16)
            nc.scalar.activation(block_b[:, :, :], block_f[:, :, :], ACT.Copy).then_inc(s_sets, 1)
            act.wait_ge(s_sm, 1)
            nc.scalar.activation(e0[:, :], skm[:, :], ACT.Exp, scale=-1.0).then_inc(s_e, 1)
            nc.scalar.activation(e1[:, :], skp[:, :], ACT.Exp).then_inc(s_e, 1)
            for g in ours(0, G_V, 4):
                values(act, nc.scalar.copy, s_eva, g)
            if by_scalar[G_FS]:
                evac(G_FS, fscale[:, :], gbank(G_FS)[:, 0:1], 1.0 / (HID * HID))
            for g in range(5):
                act.wait_ge(s_ps, G_KT + g + 1)
                if g == 4:
                    act.wait_ge(s_setd, 1)
                nc.scalar.mul(*key_parts(g)[:2], wqk[:, 0:1]).then_inc(s_hi, 1)
            act.wait_ge(s_lo, 9)
            narrow(xcF[:, :], xcT[:, 0:P].bitcast(f32), a_xc)
            narrow(kTw[:, :, :], kT[:, :, 0:P + WIN], a_kw)
            for g in ours(0, G_WG, 8):
                evac(G_WG + g, wgT[:, :, 2 * g * P:2 * g * P + 256], two(G_WG + g))

            def output_weights():
                for g in range(8):
                    act.wait_ge(s_ps, G_WE + g + 1)
                    nc.scalar.activation(Weff[:, 0, 2 * g:2 * g + 2, :], two(G_WE + g), ACT.Copy).then_inc(s_wh, 1)

            def step(i, front, mid, proj, ffn, last_norm):
                if front:
                    for hf in range(2):
                        act.wait_ge(p_q, 2 * i + 3 + hf)
                        wait(act, d_red, 2 * i + 2)
                        nc.scalar.activation(sq[:, 8 * hf:8 * hf + 8, :],
                                             qbank(hf).rearrange("p (a d) -> p a d", d=D),
                                             ACT.Square).then_inc(a_sq, 1)
                if isinstance(i, int) and i == -1:
                    output_weights()
                if mid:
                    for u, b in enumerate((6, 4, 5, 6)):
                        c, hf = divmod(u, 2)
                        if hf == 0:
                            wait(act, g_mask, 2 * i + c - 1)
                        act.wait_ge(p_sw, 4 * i + u + 1)
                        nc.scalar.activation(E[:, c, 8 * hf:8 * hf + 8, :], bank(b).rearrange("p (a q) -> p a q", q=WIN),
                                             ACT.Tanh, scale=SCALE / CAP).then_inc(a_tanh, 1)
                    for c in range(2):
                        act.wait_ge(a_tanh, 4 * i + 2 * c + 2)
                        nc.scalar.activation(E[:, c, :, :], E[:, c, :, :], ACT.Exp, scale=CAP).then_inc(a_es, 1)
                if front:
                    act.wait_ge(p_q, 2 * i + 4)
                    narrow(xcF[:, :], xcT[:, ds((i + 2) * P, P)].bitcast(f32), a_xc)
                    if mid:
                        act.wait_ge(p_sw, 4 * i + 4)
                        at = (i + 1) * P + ((i + 1) // TPB) * WIN
                        narrow(kTw[:, :, :], kT[:, :, ds(at, P + WIN)], a_kw)
                if mid:
                    if isinstance(i, int) and i == 0:
                        evac(G_FT, wfT[:, :, :], two(G_FT))
                    act.wait_ge(d_cmax, i + 1)
                    wait(act, p_ct, 2 * i)
                    for hd in range(HEADS):
                        last = nc.scalar.activation(Ec[:, hd, :], bank(4, 2)[:, hd * NBLK:(hd + 1) * NBLK], ACT.Exp,
                                                    scale=SCALE, bias=mn[:, hd:hd + 1], accum_out=sc[:, hd:hd + 1])
                        if hd % 8 == 7:
                            last.then_inc(a_ec, 1)
                    act.wait_ge(d_cm, i + 1)
                    nc.scalar.activation(es[:, :], cm[:, :], ACT.Exp).then_inc(a_ecs, 1)
                if front:
                    for hf in range(2):
                        act.wait_ge(p_qt, 2 * i + 3 + hf)
                        narrow(qT[:, 0, 8 * hf:8 * hf + 8, :], qbank(hf).rearrange("p (a q) -> p a q", q=P), a_qt)
                if isinstance(i, int) and i == -1:
                    value_weights(act, nc.scalar.copy, s_eva, 0)
                if ffn:
                    act.wait_ge(p_xt, i - 1)
                    narrow(x1T[:, :, :], ffn_bank(mid)[:, HID:2 * HID].rearrange("p (k n) -> p k n", k=KC), a_xt)
                if mid:
                    def output_T(c):
                        act.wait_ge(p_at, 2 * i + c + 1)
                        narrow(aoT[:, 0, :, :, c, :], bank((2, 4)[c], 2).rearrange("p (a r q) -> p a r q", r=2, q=WIN), a_at)

                    output_T(0)
                    for n in range(2):
                        act.wait_ge(p_ct, 2 * i + n + 1)
                        narrow(PcT[:, 4 * n:4 * n + 4, :], bank(n).rearrange("p (a q) -> p a q", q=P), a_ct)
                    output_T(1)

            all_steps(step, act)

        @block_ctx.vector
        def _(dve):
            V_ = nc.vector
            base, since = [0], [0]

            def link(ins):
                ins.then_inc(s_chain, 1)
                since[0] += 1
                dve.wait_ge(s_chain, base[0] + since[0])

            def after_link():
                dve.wait_ge(s_chain, base[0] + since[0])

            def chained(ins):
                ins.then_inc(s_chain, 1)
                since[0] += 1

            def rsqrt_part(n, x, yv, uv, tv):
                after_link()
                if n == 0:
                    chained(V_.tensor_single_scalar(uv.bitcast(i32), x.bitcast(i32), 1, ALU.logical_shift_right))
                elif n == 1:
                    chained(V_.tensor_scalar(yv.bitcast(i32), uv.bitcast(i32), -1.0, float(0x5F3759DF), ALU.mult, ALU.add))
                elif n in (2, 5):
                    chained(V_.tensor_tensor(uv, x, yv, ALU.mult))
                elif n == 3:
                    chained(V_.scalar_tensor_tensor(uv, uv, -0.5, yv, ALU.mult, ALU.mult))
                elif n == 4:
                    chained(V_.scalar_tensor_tensor(yv, uv, 1.5, yv, ALU.add, ALU.mult))
                elif n == 6:
                    chained(V_.tensor_tensor(uv, uv, yv, ALU.mult))
                elif n == 7:
                    chained(V_.tensor_scalar(tv, uv, 0.375, -1.25, ALU.mult, ALU.add))
                elif n == 8:
                    chained(V_.tensor_tensor(uv, uv, tv, ALU.mult))
                else:
                    chained(V_.scalar_tensor_tensor(yv, uv, 1.875, yv, ALU.add, ALU.mult))

            def rsqrt(*rooms):
                for n in range(10):
                    rsqrt_part(n, *rooms)
                after_link()

            def evac(g, dst, src, scale=None):
                dve.wait_ge(s_ps, g + 1)
                if scale is None:
                    V_.tensor_copy(dst, src).then_inc(s_evd, 1)
                else:
                    V_.tensor_scalar(dst, src, scale, None, ALU.mult).then_inc(s_evd, 1)

            V_.memset(ones[:, :], 1.0).then_inc(s_id, 1)
            V_.memset(V[:, :, D:VW], 1.0)
            V_.memset(V[0:64, :, 0:D].rearrange("p (b w) d -> p b w d", b=BATCH)[:, :, 0, :], 0.0)
            V_.memset(xcT[:, NT * P:].bitcast(f32), 0.0)
            for g in ours(1, G_H, 8):
                at = (g % 4) * 256
                evac(g, hT[:, :, g // 4, at:at + 256], two(g))
            for g in ours(1, G_K, 4):
                evac(G_K + g, K[:, 4 * g:4 * g + 4, :], four(G_K + g))
            dve.wait_ge(s_sq, 1)
            link(V_.tensor_reduce(ssk[:, 0:NT], sqk, AX.X, ALU.add))
            if not by_scalar[G_CR]:
                evac(G_CR, ckr[:, :], gbank(G_CR)[:, 0:P])
            dve.wait_ge(s_hi, 1)
            V_.tensor_tensor(wqup_p[:, 1, :], wqup_s[:, :], wqup_p[:, 0, :].bitcast(f32), ALU.subtract).then_inc(s_lo, 1)
            if not by_scalar[G_CK]:
                evac(G_CK, K[:, NT, :], gbank(G_CK)[:, 0:D])
            copied(dve, G_CK)
            link(V_.tensor_tensor(sqk[:, 0, :], K[:, NT, :], K[:, NT, :], ALU.mult))
            link(V_.tensor_reduce(ssk[:, NT:], sqk[:, 0:1, :], AX.X, ALU.add))
            link(V_.tensor_scalar(nx[:, 0:NT + 1], ssk[:, :], 1.0 / D, 1e-6, ALU.mult, ALU.add))
            rsqrt(*(v[:, 0:NT + 1] for v in (nx, ny, nu, nt)))
            V_.tensor_tensor(K[:, :, :], K[:, :, :], ny[:, 0:NT + 1].unsqueeze(2).to_broadcast([P, NT + 1, D]),
                             ALU.mult).then_inc(s_ks, 1)
            dve.wait_ge(s_ks, 1)
            dve.wait_ge(s_tab, 32)
            for bt in range(BATCH):
                t = slice(bt * TPB, bt * TPB + TPB)
                chained(V_.tensor_tensor(rt1[:, t, :], K[:, t, 0:ROPE], rope_s[:, :, 0:ROPE], ALU.mult))
            after_link()
            for g in range(4):
                dve.wait_ge(s_hi, g + 2)
                V_.tensor_tensor(xcT[QC:P, g * 512:(g + 1) * 512], gbank(G_XC + g)[0:QC, :],
                                 xcT[0:QC, g * 512:(g + 1) * 512].bitcast(f32), ALU.subtract).then_inc(s_lo, 1)
            dve.wait_ge(s_kr, 1)
            V_.tensor_tensor(K[:, 0:NT, 0:ROPE], rt1[:, :, :], rt2[:, :, :], ALU.add).then_inc(s_kn, 1)
            dve.wait_ge(s_small, 80)
            V_.tensor_reduce(fsum[:, :], fw_s[:, :, :], AX.XY, ALU.add, apply_absolute_value=True).then_inc(s_fs, 1)
            link(V_.tensor_tensor(wqk[:, :], qw[:, :], kw[:, :], ALU.mult))
            for par in range(2):
                rows = slice(par * 64, par * 64 + 64)
                sk = sinkb[rows, :].rearrange("p (a r) -> p r a", r=2)[:, par, :]
                V_.tensor_scalar(skm[rows, :], sk, 0.0, None, ALU.max)
                link(V_.tensor_copy(dn[rows, :], sk))
            link(V_.tensor_tensor(skp[:, :], dn[:, :], skm[:, :], ALU.subtract))
            V_.tensor_copy(skp[:, 0:1], skp[:, 0:1]).then_inc(s_sm, 1)
            link(V_.tensor_scalar(sinkr[:, :], sinkb[:, :], 1.0 / SCALE, None, ALU.mult))
            for g in ours(1, G_V, 4):
                values(dve, V_.tensor_copy, s_evd, g)
            if not by_scalar[G_FS]:
                evac(G_FS, fscale[:, :], gbank(G_FS)[:, 0:1], 1.0 / (HID * HID))
            for g in range(4):
                dve.wait_ge(s_hi, 6 + g)
                hi, src, lo = key_parts(g)
                V_.scalar_tensor_tensor(lo, src, wqk[:, 0:1], hi, ALU.mult, ALU.subtract).then_inc(s_lo, 1)
            dve.wait_ge(s_ps, G_CKT + 1)
            hi, src, lo = key_parts(4)
            link(V_.tensor_scalar(ckTv[:, 0, :], src, kw[:, 0:1], None, ALU.mult))
            V_.scalar_tensor_tensor(ckTv[:, 1, :], src, kw[:, 0:1], ckTv[:, 0, :].bitcast(f32), ALU.mult,
                                    ALU.subtract).then_inc(s_setd, 1)
            dve.wait_ge(s_hi, 10)
            V_.scalar_tensor_tensor(lo, src, wqk[:, 0:1], hi, ALU.mult, ALU.subtract).then_inc(s_lo, 1)
            for g in ours(1, G_WG, 8):
                evac(G_WG + g, wgT[:, :, 2 * g * P:2 * g * P + 256], two(G_WG + g))
            copied(dve, G_FS)
            link(V_.tensor_scalar(fthr[:, :], fscale[:, :], 1e-10, 0.5, ALU.add, ALU.mult))
            link(V_.tensor_scalar(fthn[:, :], fthr[:, :], -1.0, None, ALU.mult))
            V_.tensor_scalar(fw_a[:, :, :], fw_s[:, :, :], fthr[:, 0:1], fscale[:, 0:1], ALU.is_gt, ALU.mult)
            link(V_.tensor_scalar(fw_b[:, :, :], fw_s[:, :, :], fthn[:, 0:1], fscale[:, 0:1], ALU.is_lt, ALU.mult))
            V_.tensor_tensor(wfT[:, :, :], fw_a[:, :, :], fw_b[:, :, :], ALU.subtract).then_inc(s_fw, 1)
            dve.wait_ge(s_e, 2)
            V_.memset(ny[:, :], 1.0).then_inc(s_out, 16)
            V_.memset(nu[:, :], 1.0).then_inc(s_setd, 1)
            link(V_.memset(nx[:, :], 1.0))
            base[0], since[0] = base[0] + since[0], 0

            def weights_rest(*groups):
                for g in groups:
                    dve.wait_ge(s_wh, g + 1)
                    V_.tensor_tensor(Weff[:, 1, 2 * g:2 * g + 2, :], two(G_WE + g),
                                     Weff[:, 0, 2 * g:2 * g + 2, :].bitcast(f32), ALU.subtract).then_inc(s_wl, 1)

            NORM1, NORM2 = HEADS, HEADS + 1

            def step(i, front, mid, proj, ffn, last_norm):
                first = isinstance(i, int) and i == -1
                q = [v[:, 0:HEADS + 2] for v in (nx, ny, nu, nt)]
                S = bank(4, 2).rearrange("p (a n) -> p a n", n=NBLK)
                norms = front or ffn or last_norm
                if front:
                    t = i + 1
                    for hf in range(2):
                        dve.wait_ge(a_sq, 2 * t + hf + 1)
                        V_.tensor_reduce(ssq[:, 8 * hf:8 * hf + 8], sq[:, 8 * hf:8 * hf + 8, :], AX.X, ALU.add).then_inc(d_red, 1)
                    dve.wait_ge(d_red, 2 * t + 2)
                    chained(V_.tensor_scalar(nx[:, 0:HEADS], ssq[:, :], 1.0 / D, 1e-6, ALU.mult, ALU.add))
                if norms:
                    for n in range(6):
                        rsqrt_part(n, *q)
                if mid:
                    dve.wait_ge(p_cs, i + 1)
                    chained(V_.tensor_reduce(mc[:, :], S, AX.X, ALU.max))
                    after_link()
                    chained(V_.tensor_tensor(mm[:, :], mc[:, :], sinkr[:, :], ALU.max))
                    after_link()
                    wait(dve, a_ec, 2 * i)
                    V_.tensor_scalar(mn[:, :], mm[:, :], -SCALE, None, ALU.mult).then_inc(d_cmax, 1)
                    dve.wait_ge(d_cmax, i + 1)
                    wait(dve, a_ecs, i)
                    V_.tensor_tensor(cm[:, :], sinkb[:, :], mn[:, :], ALU.add).then_inc(d_cm, 1)
                if norms:
                    for n in range(6, 10):
                        rsqrt_part(n, *q)
                    after_link()
                if first:
                    weights_rest(0, 1, 2)
                if front:
                    wait(dve, p_qt, 2 * t)
                    for hf in range(2):
                        heads = slice(8 * hf, 8 * hf + 8)
                        V_.tensor_tensor(qs[:, heads, :], qbank(hf).rearrange("p (a d) -> p a d", d=D),
                                         ny[:, heads].unsqueeze(2).to_broadcast([P, 8, D]), ALU.mult).then_inc(d_qs, 1)
                    wait(dve, d_add, 2 * t)
                    for hf in range(2):
                        heads = slice(8 * hf, 8 * hf + 8)
                        dve.wait_ge(d_qs, 2 * t + hf + 1)
                        tab = rope_s[:, ds(t % TPB, 1), :]
                        V_.tensor_tensor(rt1[:, heads, :], qs[:, heads, 0:ROPE], tab[:, :, 0:64].to_broadcast([P, 8, 64]),
                                         ALU.mult).then_inc(d_rope, 1)
                if first:
                    weights_rest(3, 4)
                if front:
                    for hf in range(2):
                        heads = slice(8 * hf, 8 * hf + 8)
                        dve.wait_ge(d_rope, 2 * t + hf + 1)
                        dve.wait_ge(g_rt, 2 * t + hf + 1)
                        V_.tensor_tensor(qs[:, heads, 0:ROPE], rt1[:, heads, :], rt2[:, heads, :], ALU.add).then_inc(d_add, 1)
                if first:
                    weights_rest(5, 6, 7)

                def divide(c):
                    dve.wait_ge(p_pv, 2 * i + c + 1)
                    full = bank(4, 4).rearrange("p (k x) -> p k x", x=1024)[:, :, 0:3 * VW].rearrange("p k (n d) -> p k n d", d=VW)
                    third = bank(5)[:, 0:2 * VW].rearrange("p (n d) -> p n d", d=VW)

                    def split(x):
                        return x[:, 0:6].rearrange("p (k n) -> p k n", k=2), x[:, 6:8]

                    for pv, d, e in zip((full[:, :, :, D], third[:, :, D]), split(dn), split(e0)):
                        chained(V_.tensor_tensor(d, pv, e, ALU.mult))
                    if c == 0:
                        dve.wait_ge(a_ec, 2 * i + 2)
                        dve.wait_ge(a_ecs, i + 1)
                        chained(V_.tensor_tensor(dc[:, :], sc[:, :], es[:, :], ALU.add))
                    after_link()
                    chained(V_.tensor_tensor(dn2[:, :], dn[:, :], e1[:, :], ALU.add))
                    if c == 0:
                        wait(dve, g_cn, i)
                        V_.reciprocal(rc[:, :], dc[:, :]).then_inc(d_rc, 1)
                    after_link()
                    link(V_.reciprocal(dn3[:, :], dn2[:, :]))
                    link(V_.tensor_tensor(r8[:, :], dn3[:, :], e0[:, :], ALU.mult))
                    wait(dve, p_at, 2 * i + c - 1)
                    for o, pv, r in ((ao[:, c, 0:6, :].rearrange("p (k n) d -> p k n d", k=2), full[:, :, :, 0:D],
                                      split(r8)[0].unsqueeze(3).to_broadcast([P, 2, 3, D])),
                                     (ao[:, c, 6:8, :], third[:, :, 0:D], split(r8)[1].unsqueeze(2).to_broadcast([P, 2, D]))):
                        last = V_.tensor_tensor(o, pv, r, ALU.mult)
                    last.then_inc(d_ao, 1)
                    dve.wait_ge(d_ao, 2 * i + c + 1)

                def output_rest(c):
                    dve.wait_ge(a_at, 2 * i + c + 1)
                    V_.tensor_tensor(aoT[:, 1, :, :, c, :], bank((2, 4)[c], 2).rearrange("p (a r q) -> p a r q", r=2, q=WIN),
                                     aoT[:, 0, :, :, c, :].bitcast(f32), ALU.subtract).then_inc(d_al, 1)

                if mid:
                    divide(0)
                if ffn:
                    wait(dve, p_xt, i - 2)
                    V_.tensor_scalar(x1[:, :], y[:, :], mv[:, 0, 0:1], ny[:, NORM1:NORM1 + 1], ALU.subtract,
                                     ALU.mult).then_inc(d_x1, 1)
                if front:
                    for hf in range(2):
                        heads = slice(8 * hf, 8 * hf + 8)
                        dve.wait_ge(a_qt, 2 * i + 3 + hf)
                        V_.tensor_tensor(qT[:, 1, heads, :], qbank(hf).rearrange("p (a q) -> p a q", q=P),
                                         qT[:, 0, heads, :], ALU.subtract).then_inc(d_ql, 1)
                if isinstance(i, int) and i == -1:
                    value_weights(dve, V_.tensor_copy, s_evd, 1)
                def projected():
                    dve.wait_ge(p_o, i)
                    if ffn:
                        dve.wait_ge(d_x1, i - 1)
                    V_.tensor_tensor(y[:, :], bank(7)[:, 0:HID], H[:, ds(i - 1, 1), :].rearrange("p a n -> p (a n)"),
                                     ALU.add).then_inc(d_y, 1)

                if proj and mid:
                    projected()
                if last_norm:
                    t3 = i - 3
                    dve.wait_ge(s_out, 16 * t3 + 16)
                    V_.tensor_scalar(res[:, :], z[:, :], mv[:, 1, 0:1], ny[:, NORM2:NORM2 + 1], ALU.subtract,
                                     ALU.mult).then_inc(d_out, 1)
                if mid:
                    divide(1)
                    output_rest(0)
                if ffn:
                    dve.wait_ge(p_f, i - 1)
                    dve.wait_ge(g_xb, i - 1)
                    if last_norm:
                        dve.wait_ge(d_out, i - 2)
                    V_.tensor_tensor(z[:, :], ffn_bank(mid)[:, HID:2 * HID], x1b, ALU.add).then_inc(d_fr, 1)
                if mid and not front:
                    output_rest(1)
                if ffn and not mid:
                    dve.wait_ge(d_fr, i - 1)
                    chained(V_.bn_stats(bns[:, 1, :], z[:, :]))
                if proj and not mid:
                    projected()
                if proj:
                    dve.wait_ge(d_y, i)
                    chained(V_.bn_stats(bns[:, 0, :], y[:, :]))
                if ffn and mid:
                    dve.wait_ge(d_fr, i - 1)
                    chained(V_.bn_stats(bns[:, 1, :], z[:, :]))
                if proj or ffn:
                    after_link()
                    V_.memset(nu[:, 0:1], 0.0)
                    sets = slice(0 if proj else 1, 2 if ffn else 1)
                    for n in range(sets.start, sets.stop):
                        chained(V_.bn_aggr(mv[:, n, :], bns[:, n, :]))
                if mid and front:
                    output_rest(1)
                if proj or ffn:
                    after_link()
                    chained(V_.tensor_scalar(nx[:, HEADS + sets.start:HEADS + sets.stop], mv[:, sets, 1], 1e-5, None, ALU.add))
                    after_link()
            LINKS = 1 + 10 + 2 + 6 + 5 + 2 + 2 + 1

            def counted(i, *stages):
                if isinstance(i, int):
                    step(i, *stages)
                    base[0], since[0] = base[0] + since[0], 0
                    return
                before = base[0]
                base[0] = before + (i - 3) * LINKS
                step(i, *stages)
                assert since[0] == LINKS, since[0]
                base[0], since[0] = before + (NT - 4) * LINKS, 0

            all_steps(counted, dve)

        @block_ctx.gpsimd
        def _(pool):
            G = nc.gpsimd
            G.memset(ident[:, :], 0.0).then_inc(s_setp, 1)
            for bt in range(BATCH):
                last = G.memset(kT[:, :, bt * SPAN:bt * SPAN + WIN], 0.0)
            last.then_inc(s_setp, 1)
            pool.wait_ge(s_setp, 2)
            G.affine_select(out=ident[:, :], in_=ident[:, :], compare_op=ALU.not_equal, fill=1.0,
                            base=0, pattern=[[-1, P]], channel_multiplier=1).then_inc(s_id, 1)
            pool.wait_ge(s_id, 2)
            G.tensor_copy(identb[:, :], ident[:, :]).then_inc(s_setp, 1)
            pool.wait_ge(s_tab, 32)
            pool.wait_ge(s_ks, 1)
            for bt in range(BATCH):
                t = slice(bt * TPB, bt * TPB + TPB)
                G.tensor_tensor(rt2[:, t, 0:32], K[:, t, 32:64], rope_s[:, :, 64:96], ALU.mult)
                last = G.tensor_tensor(rt2[:, t, 32:64], K[:, t, 0:32], rope_s[:, :, 96:128], ALU.mult)
            last.then_inc(s_kr, 1)

            def step(i, front, mid, proj, ffn, last_norm):
                def mask(c):
                    pool.wait_ge(a_es, 2 * i + c + 1)
                    if c == 0 and front:
                        pool.wait_ge(d_red, 2 * i + 4)
                    wait(pool, p_pv, 2 * i + c - 1)
                    keep = window_s[:, 1:2, :] if c else window_s[:, ds(i % TPB, 1), :]
                    G.tensor_tensor(Pm[:, c, :, :], E[:, c, :, :], keep.to_broadcast([P, HEADS, WIN]),
                                    ALU.mult).then_inc(g_mask, 1)

                if mid:
                    mask(0)
                if front:
                    for hf in range(2):
                        heads = slice(8 * hf, 8 * hf + 8)
                        pool.wait_ge(d_qs, 2 * i + 3 + hf)
                        if hf == 0:
                            tab = rope_s[:, ds((i + 1) % TPB, 1), :]
                        else:
                            G.tensor_tensor(spare[:, :], e0[:, 0:1], e0[:, 0:1], ALU.mult)
                        G.tensor_tensor(rt2[:, heads, 0:32], qs[:, heads, 32:64], tab[:, :, 64:96].to_broadcast([P, 8, 32]),
                                        ALU.mult)
                        G.tensor_tensor(rt2[:, heads, 32:64], qs[:, heads, 0:32], tab[:, :, 96:128].to_broadcast([P, 8, 32]),
                                        ALU.mult).then_inc(g_rt, 1)
                if mid:
                    mask(1)
                    pool.wait_ge(d_rc, i + 1)
                    wait(pool, p_ct, 2 * i)
                    G.tensor_tensor(Ec[:, :, :], Ec[:, :, :], rc[:, :].unsqueeze(2).to_broadcast([P, HEADS, NBLK]),
                                    ALU.mult).then_inc(g_cn, 1)
                if ffn:
                    pool.wait_ge(d_x1, i - 1)
                    wait(pool, d_fr, i - 2)
                    G.tensor_tensor(x1b, x1[:, :], fb_s[:, :], ALU.add).then_inc(g_xb, 1)

            all_steps(step, pool)


_INS = ["L0_attn_h", "L0_attn_Wq_c", "L0_attn_Wq_up", "L0_attn_Wk", "L0_attn_Wv", "L0_attn_W_comp",
        "L0_attn_q_norm_w", "L0_attn_k_norm_w", "L0_attn_sink", "L0_attn_Wg", "L0_attn_Wo",
        "L0_ffn_weight", "L0_ffn_bias"]


def kernel(**inputs):
    import numpy as _np
    import concourse.bacc as _bacc
    from concourse import mybir as _mybir
    from concourse.bass_utils import run_bass_kernel_spmd as _run

    nc = _bacc.Bacc("TRN2", target_bir_lowering=False, num_devices=1)
    arrays = {f"in_{n}": _np.ascontiguousarray(inputs[n]) for n in _INS}
    for name, table in zip(("rope", "block", "window"), shape_tables()):
        arrays[f"table_{name}"] = table
    args = [nc.dram_tensor(n, a.shape, _mybir.dt.from_np(a.dtype), kind="ExternalInput").ap()
            for n, a in arrays.items()]
    out = nc.dram_tensor("out", (BATCH, SEQ, HID), _mybir.dt.float32, kind="ExternalOutput").ap()
    build(nc, *args, out)
    return _run(nc, [arrays], core_ids=[0]).results[0]["out"]
```
